# Optimizing a Trainium2 kernel written in Bass

```python
import numpy as np
import jax
import jax.numpy as jnp

def _softmax(x, axis=-1):
    return jax.nn.softmax(x, axis=axis)

def _gelu(x):
    return jax.nn.gelu(x, approximate=True)

def _silu(x):
    return jax.nn.silu(x)

def _sigmoid(x):
    return jax.nn.sigmoid(x)

def _layernorm(x, axis=-1, eps=1e-05):
    m = jnp.mean(x, axis=axis, keepdims=True)
    v = jnp.var(x, axis=axis, keepdims=True)
    return (x - m) / jnp.sqrt(v + eps)

def _scatter_add(tgt, idx, src, axis=0):
    return tgt.at[idx].add(src)

def _segment_sum(src, seg, n):
    return jax.ops.segment_sum(src, seg, n)
kernel_name = 'mk_gnn_preln_d2_gnn_r64_8ac063'

def setup_inputs(seed: int=0):
    np.random.seed(seed)
    _w = jnp.asarray

    def _rec_inputs():
        import jax
        import jax.numpy as jnp
        _gk = jax.random.key(seed)
        x = -0.0003713 + 1 * jax.random.normal(jax.random.fold_in(_gk, 1), (100000, 128), jnp.float32)
        src = jax.random.randint(jax.random.fold_in(_gk, 2), (25000,), 0, 100000, jnp.int32)
        dst = jax.random.randint(jax.random.fold_in(_gk, 3), (25000,), 0, 100000, jnp.int32)
        _o = jnp.argsort(dst, stable=True)
        src = src[_o]
        dst = dst[_o]
        edge_attr_32 = 0.000189758 + 1.00013 * jax.random.normal(jax.random.fold_in(_gk, 12), (25000, 32), jnp.float32)
        edge_weight = jax.random.uniform(jax.random.fold_in(_gk, 14), (25000,), jnp.float32, 0.0, 1)
        return (x, src, dst, edge_attr_32, edge_weight)
    x, src, dst, edge_attr_32, edge_weight = _rec_inputs()

    def _L0_gnn_setup():
        import jax, jax.numpy as jnp
        import numpy as np
        N = 100000
        E = 25000
        H = 8
        C = 16
        DIM = 128
        EDGE_DIM = 32
        key = jax.random.key(seed)
        ks = jax.random.split(key, 7)
        s = 1.0 / np.sqrt(DIM)
        return {'x': jax.random.normal(ks[0], (N, DIM), dtype=jnp.float32), 'edge_index': jax.random.randint(ks[1], (2, E), 0, N, dtype=jnp.int32), 'edge_attr': jax.random.normal(ks[2], (E, EDGE_DIM), dtype=jnp.float32), 'Wq': jax.random.normal(ks[3], (H * C, DIM), dtype=jnp.float32) * s, 'Wk': jax.random.normal(ks[4], (H * C, DIM), dtype=jnp.float32) * s, 'Wv': jax.random.normal(ks[5], (H * C, DIM), dtype=jnp.float32) * s, 'We': jax.random.normal(ks[6], (H, EDGE_DIM), dtype=jnp.float32) * (1.0 / np.sqrt(EDGE_DIM))}
    _L0_gnn_all = _L0_gnn_setup()
    _L0_gnn_in = {k: v for k, v in _L0_gnn_all.items() if k in ('Wq', 'Wk', 'Wv', 'We')}
    del _L0_gnn_all

    def _L1_gnn_setup():
        import jax, jax.numpy as jnp
        import numpy as np
        N_NODES = 50000
        N_EDGES = 12500
        HID = 128
        key = jax.random.key(seed)
        ks = jax.random.split(key, 10)
        s_msg = 1.0 / np.sqrt(2 * HID + 1)
        s_u1 = 1.0 / np.sqrt(2 * HID)
        s_u2 = 1.0 / np.sqrt(HID)
        return {'z': jax.random.normal(ks[0], (N_NODES, HID), dtype=jnp.float32), 'edge_weight': jax.random.uniform(ks[1], (N_EDGES,), dtype=jnp.float32), 'edge_src': jax.random.randint(ks[2], (N_EDGES,), 0, N_NODES), 'edge_dst': jax.random.randint(ks[3], (N_EDGES,), 0, N_NODES), 'Wm': jax.random.normal(ks[4], (2 * HID + 1, HID), dtype=jnp.float32) * s_msg, 'bm': jax.random.normal(ks[5], (HID,), dtype=jnp.float32) * s_msg, 'W1': jax.random.normal(ks[6], (2 * HID, HID), dtype=jnp.float32) * s_u1, 'b1': jax.random.normal(ks[7], (HID,), dtype=jnp.float32) * s_u1, 'W2': jax.random.normal(ks[8], (HID, HID), dtype=jnp.float32) * s_u2, 'b2': jax.random.normal(ks[9], (HID,), dtype=jnp.float32) * s_u2}
    _L1_gnn_all = _L1_gnn_setup()
    _L1_gnn_in = {k: v for k, v in _L1_gnn_all.items() if k in ('Wm', 'bm', 'W1', 'b1', 'W2', 'b2')}
    del _L1_gnn_all
    return {'x': x, 'src': src, 'dst': dst, 'edge_attr_32': edge_attr_32, 'edge_weight': edge_weight, 'L0_gnn_Wq': _L0_gnn_in['Wq'], 'L0_gnn_Wk': _L0_gnn_in['Wk'], 'L0_gnn_Wv': _L0_gnn_in['Wv'], 'L0_gnn_We': _L0_gnn_in['We'], 'L1_gnn_Wm': _L1_gnn_in['Wm'], 'L1_gnn_bm': _L1_gnn_in['bm'], 'L1_gnn_W1': _L1_gnn_in['W1'], 'L1_gnn_b1': _L1_gnn_in['b1'], 'L1_gnn_W2': _L1_gnn_in['W2'], 'L1_gnn_b2': _L1_gnn_in['b2']}

def reference(x, src, dst, edge_attr_32, edge_weight, L0_gnn_Wq, L0_gnn_Wk, L0_gnn_Wv, L0_gnn_We, L1_gnn_Wm, L1_gnn_bm, L1_gnn_W1, L1_gnn_b1, L1_gnn_W2, L1_gnn_b2):
    import jax
    import jax.numpy as jnp

    def _L0_gnn_ref(x, edge_index, edge_attr, Wq, Wk, Wv, We):
        import jax, jax.numpy as jnp
        import numpy as np
        N = 100000
        E = 25000
        H = 8
        C = 16
        DIM = 128
        EDGE_DIM = 32
        q = (x @ Wq.T).reshape(N, H, C)
        k = (x @ Wk.T).reshape(N, H, C)
        v = (x @ Wv.T).reshape(N, H, C)
        src, dst = (edge_index[0], edge_index[1])
        edge_bias = edge_attr @ We.T
        scores = jnp.einsum('ehc,ehc->eh', q[dst], k[src]) / np.sqrt(C) + edge_bias
        seg_max = jax.ops.segment_max(scores, dst, num_segments=N)
        ex = jnp.exp(scores - seg_max[dst])
        denom = jax.ops.segment_sum(ex, dst, num_segments=N)
        alpha = ex / denom[dst]
        msgs = v[src] * alpha[:, :, None]
        out = jax.ops.segment_sum(msgs, dst, num_segments=N)
        return out.reshape(N, H * C)

    def _L1_gnn_ref(z, edge_weight, edge_src, edge_dst, Wm, bm, W1, b1, W2, b2):
        import jax, jax.numpy as jnp
        import numpy as np
        N_NODES = 50000
        N_EDGES = 12500
        HID = 128
        n, H = z.shape
        Wd, Ws, ww = (Wm[:H], Wm[H:2 * H], Wm[2 * H])
        msgs = z[edge_dst] @ Wd + z[edge_src] @ Ws + edge_weight[:, None] * ww[None, :] + bm
        agg = jax.ops.segment_max(msgs, edge_dst, num_segments=n)
        deg = jax.ops.segment_sum(jnp.ones_like(edge_weight), edge_dst, num_segments=n)
        agg = jnp.where(deg[:, None] > 0, agg, jnp.zeros((), dtype=z.dtype))
        W1a, W1b = (W1[:H], W1[H:])
        hidden = jax.nn.relu(z @ W1a + agg @ W1b + b1)
        return hidden @ W2 + b2
    edge_index = jnp.stack([src, dst])
    h = jnp.maximum(_layernorm(x, axis=-1), 0.0)
    x = x + _L0_gnn_ref(h, edge_index, edge_attr_32, L0_gnn_Wq, L0_gnn_Wk, L0_gnn_Wv, L0_gnn_We)
    h = jnp.maximum(_layernorm(x, axis=-1), 0.0)
    x = x + _L1_gnn_ref(h, edge_weight, src, dst, L1_gnn_Wm, L1_gnn_bm, L1_gnn_W1, L1_gnn_b1, L1_gnn_W2, L1_gnn_b2)
    return x

_drawn_inputs = setup_inputs


def setup_inputs(seed=0):
    import zlib

    import numpy as np

    out = dict(_drawn_inputs(seed))
    spreads = {}
    factors = {'edge_weight': 8.0,
     'L0_gnn_Wq': 4.004,
     'L0_gnn_Wk': 4.026,
     'L1_gnn_bm': 3.38,
     'edge_attr_32': 3.776,
     'L0_gnn_We': 3.772}
    for name, (base, spread) in spreads.items():
        noise = np.random.default_rng([zlib.crc32(name.encode()), seed]).standard_normal(out[name].shape)
        drawn = base * np.exp(spread * noise) if base else spread * noise
        out[name] = jnp.asarray(drawn.astype(out[name].dtype))
    for name, factor in factors.items():
        out[name] = (out[name] * factor).astype(out[name].dtype)
    return out
```

```python
from contextlib import ExitStack

import numpy as np

import concourse.bass as bass
from concourse import mybir

F32 = mybir.dt.float32
BF16 = mybir.dt.bfloat16
I32 = mybir.dt.int32
U32 = mybir.dt.uint32
ALU = mybir.AluOpType
ACT = mybir.ActivationFunctionType

P = 128
D = 128
HEADS = 8
CH = D // HEADS
KA = 32
ET = 4
EC = ET * P
NT = 16
NCH = NT * P
DT = NT // ET
NL = NT + 2 * ET
ACT_TILES = 8
EPS = 1e-5
NEG = -3.0e38
NO_ROW = 1 << 20


class Step:

    def __init__(self, i, par, last, n_edges, n_nodes):
        self.i, self.par, self.last = i, par, last
        self.c = i * 2 + par
        self.edge0 = n_edges - EC if last else i * (2 * EC) + par * EC
        self.node0 = n_nodes - NCH if last else i * (2 * NCH) + par * NCH

    def edges(self):
        return bass.ds(self.edge0, EC)

    def nodes(self):
        return bass.ds(self.node0, NCH)


def gnn_two_layers(nc, x, src, dst, edge_attr, edge_weight, Wq, Wk, Wv, We, Wm, bm, W1, b1, W2, b2, out):
    N, E = x.shape[0], src.shape[0]
    STEPS = -(-E // EC)
    assert STEPS == -(-N // NCH) and STEPS % 2 == 1
    FULL = STEPS - 1
    LOOPS = (FULL - 2) // 2
    EPP = E // 125

    def step(c, k=0):
        if isinstance(c, Step):
            if isinstance(c.i, int):
                return step(c.c + k)
            p = c.par + k
            return Step(c.i + p // 2, p % 2, False, E, N)
        n = c + k
        return Step(n // 2, n % 2, n == FULL, E, N) if n <= FULL else None

    def run(eng, body):
        with eng.Fori(0, LOOPS) as i:
            for par in range(2):
                body(Step(i, par, False, E, N))
        for c in range(2 * LOOPS, STEPS):
            body(step(c))

    with ExitStack() as ctx:
        def sb(name, shape, dt=F32):
            return ctx.enter_context(nc.sbuf_tensor(name, shape, dt))

        def sem(name):
            return ctx.enter_context(nc.semaphore(name))

        def sem2(name):
            return [sem(f"{name}_{p}") for p in range(2)]

        bank = [ctx.enter_context(nc.psum_tensor(f"bank{b}", [P, 512], F32)) for b in range(8)]
        T_ps, H_ps, O_ps, E0, E1, E2, E3, E4 = bank

        restart_row = nc.dram_tensor("restart_row", [E], F32).ap()
        last_edge = nc.dram_tensor("last_edge", [N, 1], I32).ap()
        xs_rows = nc.dram_tensor("xs_rows", [E, D], F32).ap()
        x1_rows = nc.dram_tensor("x1_rows", [E, D], F32).ap()

        ident = sb("ident", [P, P])
        head_sum = sb("head_sum", [P, P])
        wload = sb("wload", [P, 4, P])
        we_rows = sb("we_rows", [P, ET, KA])
        WqT, WkT, WvT, WdT = (sb(n, [P, P]) for n in ("WqT", "WkT", "WvT", "WdT"))
        WeT = sb("WeT", [P, ET, P])
        Ws = sb("Ws", [P, P])
        W1a, W1b, W2s, Wh = (sb(n, [P, P]) for n in ("W1a", "W1b", "W2s", "Wh"))
        cols = sb("cols", [P, 4])
        b2_rep = sb("b2_rep", [P, 512])
        b2_part = sb("b2_part", [P, 3, 512], BF16)
        b2_rest = sb("b2_rest", [P, 2, 512])
        b2_rows = sb("b2_rows", [P, 512], BF16)
        ones_bf = sb("ones_bf", [P, P], BF16)
        neg_half = sb("neg_half", [P, NL])

        src_i = sb("src_i", [P, STEPS, ET], I32)
        dst_i = sb("dst_i", [P, STEPS, ET], I32)
        next_i = sb("next_i", [P, STEPS, ET], I32)
        inner = sb("inner", [P, STEPS, ET])
        end_i = sb("end_i", [P, STEPS, ET], I32)
        edge_i = sb("edge_i", [P, STEPS, ET], I32)
        found = sb("found", [P, STEPS, ET], I32)
        dst_l = sb("dst_l", [125, EPP], I32)
        prev_l = sb("prev_l", [125, EPP], I32)
        restart_l = sb("restart_l", [125, EPP])
        no_rows = sb("no_rows", [125, N // 125], I32)
        gather_ix = sb("gather_ix", [P, 2, 2, ET], I32)
        table_ix = sb("table_ix", [P, 2, 2, 2 * ET], I32)
        table_got = sb("table_got", [P, 2, 2 * ET], I32)

        x_in = sb("x_in", [P, 2, NT, D])
        x_out = sb("x_out", [P, 2, NT, D])
        h = sb("h", [P, 2, NL, D])
        xs = sb("xs", [P, 2, ET, D])
        xd = sb("xd", [P, 2, ET, D])
        xd_kept = sb("xd_kept", [P, 2, ET, D])
        x1 = sb("x1", [P, 2, ET, D])
        attr = sb("attr", [P, 2, ET, KA])
        restart = sb("restart", [P, 2, EC])
        ew = sb("ew", [P, 2, EC])
        stats = sb("stats", [P, NL, 6])
        sums, diff, q4, sq, var, rstd, shift = (sb(n, [P, NL]) for n in
                                               ("sums", "diff", "q4", "sq", "var", "rstd", "shift"))
        hsT, hdT, q_sb, qk, s_sb = (sb(n, [P, EC]) for n in ("hsT", "hdT", "q_sb", "qk", "s_sb"))
        attrT = sb("attrT", [P, P])
        ga, gb, bv = (sb(n, [P, EC]) for n in ("ga", "gb", "bv"))
        den = sb("den", [P, 2, EC])
        rden, att = (sb(n, [P, EC]) for n in ("rden", "att"))
        carry = sb("carry", [P, 2])
        hT = sb("hT", [P, 2, 512])
        hid = sb("hid", [P, 2, 512])
        msg = sb("msg", [P, EC])
        top = sb("top", [P, 2, EC])
        hidB = sb("hidB", [P, EC])

        w_in, col_in, b2_in, ix_in, l_in, ew_in0 = (sem(n) for n in
                                                    ("w_in", "col_in", "b2_in", "ix_in", "l_in", "ew_in0"))
        consts_pool, consts_dve = sem("consts_pool"), sem("consts_dve")
        setup_ps, setup_sb = sem("setup_ps"), sem("setup_sb")
        b2_split = sem("b2_split")
        restart_ready, restart_stored = sem("restart_ready"), sem("restart_stored")
        ends_ready, table_cleared = sem("ends_ready"), sem("table_cleared")
        no_rows_ready, ends_found = sem("no_rows_ready"), sem("ends_found")
        x_loaded, attr_loaded, restart_loaded = sem2("x_loaded"), sem2("attr_loaded"), sem2("restart_loaded")
        xs_got, xd_got = sem2("xs_got"), sem2("xd_got")
        xs_stored, x1_stored, out_stored = sem2("xs_stored"), sem2("x1_stored"), sem2("out_stored")
        table_put, table_read = sem2("table_put"), sem2("table_read")
        ys_loaded, yd_loaded, ew_loaded, restartB_loaded = (sem2(n) for n in
                                                            ("ys_loaded", "yd_loaded", "ew_loaded", "restartB_loaded"))
        ys_replaced, out_put = sem2("ys_replaced"), sem2("out_put")
        gate, sp_gate = sem("gate"), sem("sp_gate")
        ix_staged, table_staged, found_kept = sem("ix_staged"), sem("table_staged"), sem("found_kept")
        ln = sem("ln")
        var_ready, rstd_ready, shift_ready = sem("var_ready"), sem("rstd_ready"), sem("shift_ready")
        normed_dve, normed_act, xd_copied = sem("normed_dve"), sem("normed_act"), sem("xd_copied")
        hsT_ps, hdT_ps, attrT_ps, q_ps, k_ps, v_ps, s_ps, att_ps = (sem(n) for n in
            ("hsT_ps", "hdT_ps", "attrT_ps", "q_ps", "k_ps", "v_ps", "s_ps", "att_ps"))
        hsT_ok, hdT_ok, attrT_ok, q_ok, s_ok = (sem(n) for n in ("hsT_ok", "hdT_ok", "attrT_ok", "q_ok", "s_ok"))
        hT_ps, hid_ps, o_ps, hT_ok, hid_ok, out_ok = (sem(n) for n in
            ("hT_ps", "hid_ps", "o_ps", "hT_ok", "hid_ok", "out_ok"))
        qk_ok, max_ok, gap0_ok, gaps_ok, carried = (sem(n) for n in ("qk_ok", "max_ok", "gap0_ok", "gaps_ok", "carried"))
        exp_ok, den_ok, bv_ok, sum_ok, rden_ok, att_ok, x1_ok = (sem(n) for n in
            ("exp_ok", "den_ok", "bv_ok", "sum_ok", "rden_ok", "att_ok", "x1_ok"))
        phaseA_stored = sem("phaseA_stored")
        varB, rstdB, shiftB, normedB, lnB = (sem(n) for n in ("varB", "rstdB", "shiftB", "normedB", "lnB"))
        ysT_ps, ydT_ps, m_ps, g_ps, r_ps = (sem(n) for n in ("ysT_ps", "ydT_ps", "m_ps", "g_ps", "r_ps"))
        ysT_ok, ydT_ok, msg_ok, top_ok, g_ok, row_ok = (sem(n) for n in
            ("ysT_ok", "ydT_ok", "msg_ok", "top_ok", "g_ok", "row_ok"))
        ixB_staged, endB_staged = sem("ixB_staged"), sem("endB_staged")

        attr_v = lambda s: edge_attr[s.edges(), :].rearrange("(p j) k -> p j k", j=ET)
        rows_v = lambda t, s: t[s.edges(), :].rearrange("(p j) d -> p j d", j=ET)
        nodes_v = lambda t, s: t[s.nodes(), :].rearrange("(p j) d -> p j d", j=NT)
        spread = lambda t, s: t[s.edges()].partition_broadcast(P)

        block = ctx.enter_context(nc.Block())

        @block.sync
        def _(sp):
            def load_node_rows(s):
                sp.dma_start(x_in[:, s.par], nodes_v(x, s)).then_inc(x_loaded[s.par], 16)

            def load_attr(s):
                sp.dma_start(attr[:, s.par], attr_v(s)).then_inc(attr_loaded[s.par], 16)

            def load_restart(s, done):
                sp.dma_start(restart[:, s.par], spread(restart_row, s)).then_inc(done[s.par], 16)

            full = FULL * EC
            for tile_, a in ((src_i, src), (dst_i, dst)):
                sp.dma_start(tile_[:, 0:FULL, :], a[0:full].rearrange("(c p j) -> p c j", p=P, j=ET)).then_inc(ix_in, 16)
                sp.dma_start(tile_[:, FULL, :], a[E - EC:E].rearrange("(p j) -> p j", j=ET)).then_inc(ix_in, 16)
            sp.dma_start(dst_l[:, :], dst.rearrange("(p j) -> p j", p=125)).then_inc(l_in, 16)
            sp.wait_ge(consts_pool, 1)
            sp.dma_start(prev_l[0:1, 1:EPP], dst[0:EPP - 1].rearrange("(a j) -> a j", a=1)).then_inc(l_in, 16)
            sp.dma_start(prev_l[1:125, :], dst[EPP - 1:E - 1].rearrange("(p j) -> p j", j=EPP)).then_inc(l_in, 16)
            sp.dma_start(next_i[:, 0:FULL, :], dst[1:full + 1].rearrange("(c p j) -> p c j", p=P, j=ET)).then_inc(ix_in, 16)
            sp.dma_start(next_i[0:P - 1, FULL, :], dst[E - EC + 1:E - ET + 1].rearrange("(p j) -> p j", j=ET)).then_inc(ix_in, 16)
            sp.dma_start(next_i[P - 1:P, FULL, 0:ET - 1], dst[E - ET + 1:E].rearrange("(a j) -> a j", a=1)).then_inc(ix_in, 16)
            for c in range(2):
                load_node_rows(step(c))
                load_attr(step(c))
            for n, w in enumerate((Wq, Wk, Wv, Wm[0:D, :])):
                sp.dma_start(wload[:, n], w[:, :]).then_inc(w_in, 16)
            for hd in range(HEADS):
                sp.dma_start(we_rows[CH * hd:CH * (hd + 1)],
                             We[hd:hd + 1, :].unsqueeze(0).broadcast_to([CH, ET, KA])).then_inc(w_in, 16)
            sp.dma_start(Ws[:, :], Wm[D:2 * D, :]).then_inc(w_in, 16)
            sp.dma_start(W1a[:, :], W1[0:D, :]).then_inc(w_in, 16)
            sp.dma_start(W1b[:, :], W1[D:2 * D, :]).then_inc(w_in, 16)
            sp.dma_start(W2s[:, :], W2[:, :]).then_inc(w_in, 16)
            for n, v in enumerate((bm, b1, Wm[2 * D])):
                sp.dma_start(cols[:, n:n + 1], v.rearrange("(p a) -> p a", a=1)).then_inc(col_in, 16)
            sp.dma_start(b2_rep[:, 0:D], b2.partition_broadcast(P)).then_inc(b2_in, 16)
            sp.wait_ge(restart_ready, 1)
            sp.dma_start(restart_row.rearrange("(p j) -> p j", p=125), restart_l[:, :]).then_inc(restart_stored, 16)
            sp.wait_ge(no_rows_ready, 1)
            sp.dma_start(last_edge.rearrange("(p j) a -> p (j a)", p=125), no_rows[:, :]).then_inc(table_cleared, 16)
            sp.wait_ge(restart_stored, 16)
            for c in range(2):
                load_restart(step(c), restart_loaded)

            def open_gate():
                sp.sem_inc(sp_gate, 1)

            def store_xs(s):
                if s.last:
                    sp.wait_ge(xs_stored[1 - s.par], 16 * s.i)
                sp.wait_ge(xs_got[s.par], 16 * ET * (s.i + 1))
                open_gate()
                sp.dma_start(rows_v(xs_rows, s), xs[:, s.par]).then_inc(xs_stored[s.par], 16)

            store_xs(step(0))

            def phase_a(s):
                nxt, far = step(s, 1), step(s, 2)
                if nxt:
                    store_xs(nxt)
                if far:
                    sp.wait_ge(attrT_ps, s.c + 1)
                    open_gate()
                    load_attr(far)
                    sp.wait_ge(gaps_ok, s.c + 1)
                    open_gate()
                    load_restart(far, restart_loaded)
                sp.wait_ge(out_ok, DT * (s.c + 1))
                open_gate()
                if s.last:
                    sp.wait_ge(out_stored[1 - s.par], 16 * s.i)
                sp.dma_start(nodes_v(out, s), x_out[:, s.par]).then_inc(out_stored[s.par], 16)
                if far:
                    load_node_rows(far)
                sp.wait_ge(x1_ok, s.c + 1)
                open_gate()
                if s.last:
                    sp.wait_ge(x1_stored[1 - s.par], 16 * s.i)
                sp.dma_start(rows_v(x1_rows, s), x1[:, s.par]).then_inc(x1_stored[s.par], 16)

            run(sp, phase_a)

            for p in range(2):
                uses = FULL // 2 + (1 - p)
                for stored in (xs_stored, x1_stored, out_stored):
                    sp.wait_ge(stored[p], 16 * uses)
            sp.sem_inc(phaseA_stored, 1)

            def load_ys(s):
                sp.dma_start(xs[:, s.par], rows_v(xs_rows, s)).then_inc(ys_loaded[s.par], 16)

            def load_yd(s):
                sp.dma_start(xd[:, s.par], rows_v(x1_rows, s)).then_inc(yd_loaded[s.par], 16)

            def load_ew(s):
                sp.dma_start(ew[:, s.par], spread(edge_weight, s)).then_inc(ew_loaded[s.par], 16)

            for c in range(2):
                load_ys(step(c))
                load_yd(step(c))
                load_ew(step(c))
                load_restart(step(c), restartB_loaded)

            def phase_b(s):
                far = step(s, 2)
                if far:
                    sp.wait_ge(normedB, s.c + 1)
                    open_gate()
                    load_ys(far)
                    sp.wait_ge(msg_ok, s.c + 1)
                    open_gate()
                    load_ew(far)
                    sp.wait_ge(top_ok, s.c + 1)
                    open_gate()
                    load_restart(far, restartB_loaded)
                    sp.wait_ge(row_ok, s.c + 1)
                    open_gate()
                    load_yd(far)

            run(sp, phase_b)
            for p in range(2):
                uses = FULL // 2 + (1 - p)
                sp.wait_ge(out_put[p], 16 * ET * uses)

        @block.gpsimd
        def _(pool):
            pool.memset(prev_l[:, :], -1)
            pool.memset(next_i[:, :, :], -1).then_inc(consts_pool, 1)
            pool.memset(no_rows[:, :], NO_ROW).then_inc(no_rows_ready, 1)
            pool.memset(ident[:, :], 0.0)
            pool.memset(neg_half[:, :], -0.5)
            pool.memset(head_sum[:, :], 1.0).then_inc(consts_pool, 1)
            pool.iota(edge_i[:, 0:FULL, :], pattern=[[EC, FULL], [1, ET]], base=0, channel_multiplier=ET)
            pool.iota(edge_i[:, FULL, :], pattern=[[1, ET]], base=E - EC, channel_multiplier=ET).then_inc(consts_pool, 1)
            pool.wait_ge(consts_pool, 3)
            pool.affine_select(out=ident[:, :], in_=ident[:, :], compare_op=ALU.not_equal, fill=1.0,
                               base=0, pattern=[[-1, P]], channel_multiplier=1).then_inc(consts_pool, 1)
            blocks = head_sum[:, :].rearrange("p (g r) -> p g r", r=CH)
            pool.affine_select(out=blocks, in_=blocks, compare_op=ALU.is_ge, fill=0.0, base=0,
                               pattern=[[-CH, HEADS], [0, CH]], channel_multiplier=1).then_inc(consts_pool, 1)
            pool.wait_ge(consts_pool, 5)
            pool.affine_select(out=blocks, in_=blocks, compare_op=ALU.is_ge, fill=0.0, base=CH - 1,
                               pattern=[[CH, HEADS], [0, CH]], channel_multiplier=-1).then_inc(consts_pool, 1)

            def open_gate():
                pool.sem_inc(gate, 1)

            def gather(s, first):
                pool.wait_ge(xs_got[s.par], 16 * ET * s.i)
                pool.wait_ge(xd_got[s.par], 16 * ET * s.i)
                open_gate()
                pool.tensor_copy(gather_ix[:, s.par, 0], src_i[:, bass.ds(s.c, 1), :].rearrange("p a j -> p (a j)"))
                pool.tensor_copy(gather_ix[:, s.par, 1],
                                 dst_i[:, bass.ds(s.c, 1), :].rearrange("p a j -> p (a j)")).then_inc(ix_staged, 1)
                pool.wait_ge(ix_staged, s.c + 1)
                if not first:
                    pool.wait_ge(normed_dve, s.c - 1)
                    pool.wait_ge(normed_act, s.c - 1)
                    pool.wait_ge(xd_copied, s.c - 1)
                    pool.wait_ge(xs_stored[s.par], 16 * s.i)
                open_gate()
                for rows, which, got in ((xs, 0, xs_got), (xd, 1, xd_got)):
                    for j in range(ET):
                        pool.indirect_dma_start(
                            out=rows[:, s.par, j], out_offset=None, in_=x,
                            in_offset=bass.IndirectOffsetOnAxis(ap=gather_ix[:, s.par, which, j:j + 1].bitcast(U32), axis=0),
                        ).then_inc(got[s.par], 16)

            def inverse_roots(ready, done, s, n):
                pool.wait_ge(ready, s.c + 1)
                pool.tensor_tensor(rstd[:, 0:n], var[:, 0:n], neg_half[:, 0:n], ALU.pow).then_inc(done, 1)

            pool.wait_ge(ix_in, 7 * 16)
            gather(step(0), True)
            gather(step(1), True)
            inverse_roots(var_ready, rstd_ready, step(0), NL)

            def table_columns(a, first, width):
                return a[:, bass.ds(first, width), :].rearrange("p a j -> p (a j)")

            def put_entries(k, uses, n, first, width):
                cols_ = width * ET
                pool.wait_ge(table_put[k], 16 * uses)
                open_gate()
                pool.tensor_copy(table_ix[:, k, 0, 0:cols_], table_columns(end_i, first, width))
                pool.tensor_copy(table_ix[:, k, 1, 0:cols_], table_columns(edge_i, first, width)).then_inc(table_staged, 1)
                pool.wait_ge(table_staged, n + 1)
                open_gate()
                for j in range(cols_):
                    pool.indirect_dma_start(
                        out=last_edge, out_offset=bass.IndirectOffsetOnAxis(
                            ap=table_ix[:, k, 0, j:j + 1].bitcast(U32), axis=0),
                        in_=table_ix[:, k, 1, j:j + 1], in_offset=None,
                        bounds_check=N - 1, oob_is_err=False).then_inc(table_put[k], 16)

            def read_entries(k, uses, n, first, width):
                cols_ = width * ET
                pool.wait_ge(table_read[k], 16 * uses)
                open_gate()
                pool.tensor_copy(table_ix[:, k, 0, 0:cols_], table_columns(src_i, first, width)).then_inc(table_staged, 1)
                pool.wait_ge(table_staged, n + 1)
                open_gate()
                for j in range(cols_):
                    pool.indirect_dma_start(
                        out=table_got[:, k, j:j + 1], out_offset=None, in_=last_edge,
                        in_offset=bass.IndirectOffsetOnAxis(ap=table_ix[:, k, 0, j:j + 1].bitcast(U32), axis=0),
                    ).then_inc(table_read[k], 16)

            def keep_entries(k, uses, first, width):
                cols_ = width * ET
                pool.wait_ge(table_read[k], 16 * uses)
                open_gate()
                pool.tensor_copy(table_columns(found, first, width), table_got[:, k, 0:cols_]).then_inc(found_kept, 1)

            def phase_a(s, table_work):
                nxt, far = step(s, 1), step(s, 2)
                if far:
                    gather(far, False)
                if nxt:
                    inverse_roots(var_ready, rstd_ready, nxt, NL)
                table_work(s)

            HALF = LOOPS // 2 + 1
            put_steps = 2 * HALF

            pool.wait_ge(ends_ready, 2)
            pool.wait_ge(table_cleared, 16)

            def put_work(s):
                put_entries(s.par, 2 * ET * s.i, s.c, s.c * 2, 2)

            with pool.Fori(0, HALF) as i:
                for par in range(2):
                    phase_a(Step(i, par, False, E, N), put_work)
            left = STEPS - 2 * put_steps
            assert left == 1
            for p in range(2):
                pool.wait_ge(table_put[p], 16 * 2 * ET * HALF)
            put_entries(0, 2 * ET * HALF, put_steps, FULL, 1)
            pool.wait_ge(table_put[0], 16 * (2 * ET * HALF + ET))

            def read_work(s, base=put_steps):
                n = s.c - base
                read_entries(s.par, 2 * ET * (s.i - HALF), s.c + 1, n * 2, 2)
                keep_entries(s.par, 2 * ET * (s.i - HALF + 1), n * 2, 2)

            with pool.Fori(HALF, LOOPS) as i:
                for par in range(2):
                    phase_a(Step(i, par, False, E, N), read_work)
            for c in range(2 * LOOPS, STEPS):
                phase_a(step(c), lambda s: read_work(s) if 2 * (s.c - put_steps) < FULL else None)
            done = min(STEPS, put_steps + FULL // 2) - put_steps
            reads = [sum(1 for n in range(done) if (n + put_steps) % 2 == p) for p in range(2)]
            staged = put_steps + 1 + done
            first = 2 * done
            while first < STEPS:
                width = min(2, STEPS - first)
                k = (done + put_steps) % 2
                read_entries(k, 2 * ET * reads[k], staged, first, width)
                keep_entries(k, 2 * ET * reads[k] + width * ET, first, width)
                reads[k] += 1
                staged, done, first = staged + 1, done + 1, first + width

            def replace_rows(s):
                pool.wait_ge(ys_replaced[s.par], 16 * ET * s.i)
                open_gate()
                pool.tensor_copy(gather_ix[:, s.par, 0],
                                 found[:, bass.ds(s.c, 1), :].rearrange("p a j -> p (a j)")).then_inc(ixB_staged, 1)
                pool.wait_ge(ixB_staged, s.c + 1)
                pool.wait_ge(ys_loaded[s.par], 16 * (s.i + 1))
                open_gate()
                for j in range(ET):
                    pool.indirect_dma_start(
                        out=xs[:, s.par, j], out_offset=None, in_=x1_rows,
                        in_offset=bass.IndirectOffsetOnAxis(ap=gather_ix[:, s.par, 0, j:j + 1].bitcast(U32), axis=0),
                        bounds_check=E - 1, oob_is_err=False).then_inc(ys_replaced[s.par], 16)

            def put_rows(s):
                pool.wait_ge(out_put[s.par], 16 * ET * s.i)
                open_gate()
                pool.tensor_copy(gather_ix[:, s.par, 1],
                                 end_i[:, bass.ds(s.c, 1), :].rearrange("p a j -> p (a j)")).then_inc(endB_staged, 1)
                pool.wait_ge(endB_staged, s.c + 1)
                pool.wait_ge(row_ok, s.c + 1)
                if s.last:
                    pool.wait_ge(out_put[1 - s.par], 16 * ET * s.i)
                open_gate()
                for j in range(ET):
                    pool.indirect_dma_start(
                        out=out, out_offset=bass.IndirectOffsetOnAxis(
                            ap=gather_ix[:, s.par, 1, j:j + 1].bitcast(U32), axis=0),
                        in_=x1[:, s.par, j], in_offset=None,
                        bounds_check=N - 1, oob_is_err=False).then_inc(out_put[s.par], 16)

            pool.wait_ge(phaseA_stored, 1)
            pool.wait_ge(found_kept, done)
            open_gate()
            replace_rows(step(0))
            replace_rows(step(1))
            inverse_roots(varB, rstdB, step(0), 2 * ET)

            def phase_b(s):
                nxt, far = step(s, 1), step(s, 2)
                if nxt:
                    inverse_roots(varB, rstdB, nxt, 2 * ET)
                if far:
                    replace_rows(far)
                put_rows(s)

            run(pool, phase_b)

        @block.vector
        def _(dve):
            def row_of(s, t):
                return (x_in[:, s.par, t] if t < NT else xs[:, s.par, t - NT] if t < NT + ET
                        else xd[:, s.par, t - NT - ET])

            dve.memset(ones_bf[:, :], 1.0)
            dve.memset(b2_rows[:, :], 0.0)
            dve.memset(carry[:, :], 0.0)
            dve.memset(den[:, :, :], 0.0)
            dve.memset(top[:, :, :], 0.0)
            dve.memset(WeT[:, :, :], 0.0).then_inc(consts_dve, 1)
            dve.wait_ge(l_in, 3 * 16)
            dve.tensor_tensor(restart_l[:, :], dst_l[:, :], prev_l[:, :], ALU.not_equal).then_inc(ends_found, 1)
            dve.wait_ge(ends_found, 1)
            dve.tensor_scalar(restart_l[:, :], restart_l[:, :], NEG, None, ALU.mult).then_inc(restart_ready, 1)
            dve.wait_ge(ix_in, 7 * 16)
            dve.tensor_tensor(inner[:, :, :], dst_i[:, :, :], next_i[:, :, :], ALU.is_equal).then_inc(ends_ready, 1)
            dve.wait_ge(ends_ready, 1)
            dve.scalar_tensor_tensor(end_i[:, :, :], inner[:, :, :], float(NO_ROW), dst_i[:, :, :],
                                     ALU.mult, ALU.add).then_inc(ends_ready, 1)
            dve.wait_ge(b2_in, 16)
            for k in range(1, 4):
                dve.tensor_copy(b2_rep[:, k * D:(k + 1) * D], b2_rep[:, 0:D]).then_inc(b2_split, 1)
            dve.wait_ge(b2_split, 3)
            dve.tensor_copy(b2_part[:, 0], b2_rep[:, :]).then_inc(b2_split, 1)
            dve.wait_ge(b2_split, 4)
            dve.tensor_tensor(b2_rest[:, 0], b2_rep[:, :], b2_part[:, 0], ALU.subtract).then_inc(b2_split, 1)
            dve.wait_ge(b2_split, 5)
            dve.tensor_copy(b2_part[:, 1], b2_rest[:, 0]).then_inc(b2_split, 1)
            dve.wait_ge(b2_split, 6)
            dve.tensor_tensor(b2_rest[:, 1], b2_rest[:, 0], b2_part[:, 1], ALU.subtract).then_inc(b2_split, 1)
            dve.wait_ge(b2_split, 7)
            dve.tensor_copy(b2_part[:, 2], b2_rest[:, 1]).then_inc(b2_split, 1)
            dve.wait_ge(b2_split, 8)
            dve.wait_ge(consts_dve, 1)
            for k in range(3):
                dve.tensor_copy(b2_rows[32 * k:32 * k + 1, :], b2_part[32 * k:32 * k + 1, k]).then_inc(b2_split, 1)
            dve.wait_ge(setup_ps, 1)
            dve.tensor_scalar(WqT[:, :], E0[:, 0:P], 1.0 / np.sqrt(CH), None, ALU.mult)
            for k, w in enumerate((WkT, WvT, WdT)):
                dve.tensor_copy(w[:, :], E0[:, (k + 1) * P:(k + 2) * P])
            for j in range(ET):
                last = dve.tensor_copy(WeT[KA * j:KA * (j + 1), j], E1[KA * j:KA * (j + 1), 0:P])
            last.then_inc(setup_sb, 1)
            dve.wait_ge(setup_ps, 2)
            dve.tensor_tensor(Wh[:, :], E2[:, 0:P], W1a[:, :], ALU.add)
            dve.wait_ge(col_in, 3 * 16)
            dve.tensor_tensor(cols[:, 3:4], E3[:, 0:1], cols[:, 1:2], ALU.add).then_inc(setup_sb, 1)

            def norm_stats(s, tiles, at):
                for t in tiles:
                    ins = dve.bn_stats(stats[:, t - at], row_of(s, t))
                return ins

            def norm_scales(s, n, mine, var_done):
                m0, m1 = stats[:, 0:n, 1], stats[:, 0:n, 4]
                v0, v1 = stats[:, 0:n, 2], stats[:, 0:n, 5]
                dve.wait_ge(mine, s.c * 3 + 1)
                dve.tensor_tensor(sums[:, 0:n], m0, m1, ALU.add)
                dve.tensor_tensor(diff[:, 0:n], m0, m1, ALU.subtract)
                dve.tensor_tensor(q4[:, 0:n], v0, v1, ALU.add).then_inc(mine, 1)
                dve.wait_ge(mine, s.c * 3 + 2)
                dve.scalar_tensor_tensor(sq[:, 0:n], diff[:, 0:n], 0.25, diff[:, 0:n], ALU.mult, ALU.mult)
                dve.tensor_scalar(q4[:, 0:n], q4[:, 0:n], 1.0 / D, EPS, ALU.mult, ALU.add).then_inc(mine, 1)
                dve.wait_ge(mine, s.c * 3 + 3)
                dve.tensor_tensor(var[:, 0:n], q4[:, 0:n], sq[:, 0:n], ALU.add).then_inc(var_done, 1)

            def norm_shift(s, n, rstd_done, shift_done):
                dve.wait_ge(rstd_done, s.c + 1)
                dve.scalar_tensor_tensor(shift[:, 0:n], sums[:, 0:n], -0.5, rstd[:, 0:n],
                                         ALU.mult, ALU.mult).then_inc(shift_done, 1)
                dve.wait_ge(shift_done, s.c + 1)

            def norm_rows(s, tiles, at):
                for t in tiles:
                    ins = dve.tensor_scalar(h[:, s.par, t], row_of(s, t), rstd[:, t - at:t - at + 1],
                                            shift[:, t - at:t - at + 1], ALU.mult, ALU.add)
                return ins

            dve_tiles = list(range(ACT_TILES, NL))

            def front_stats_nodes(s):
                dve.wait_ge(normed_act, s.c)
                dve.wait_ge(x_loaded[s.par], 16 * (s.i + 1))
                norm_stats(s, range(NT), 0)

            def front_stats_edges(s):
                dve.wait_ge(xs_got[s.par], 16 * ET * (s.i + 1))
                dve.wait_ge(xd_got[s.par], 16 * ET * (s.i + 1))
                norm_stats(s, range(NT, NL), 0).then_inc(ln, 1)
                norm_scales(s, NL, ln, var_ready)

            def front_rows(s, now=None):
                norm_shift(s, NL, rstd_ready, shift_ready)
                if now:
                    dve.wait_ge(hT_ps, DT * now.c)
                    dve.wait_ge(hdT_ps, now.c)
                norm_rows(s, dve_tiles, 0).then_inc(normed_dve, 1)

            front_stats_nodes(step(0))
            front_stats_edges(step(0))
            front_rows(step(0))

            def add_rows(s, k):
                if k == 0:
                    dve.wait_ge(out_stored[s.par], 16 * s.i)
                dve.wait_ge(o_ps, DT * s.c + k + 1)
                dve.tensor_tensor(x_out[:, s.par, ET * k:ET * (k + 1)],
                                  O_ps[:, :].rearrange("p (j d) -> p j d", j=ET),
                                  x_in[:, s.par, ET * k:ET * (k + 1)], ALU.add).then_inc(out_ok, 1)

            SEAM = FULL * EC - (E - EC)

            def phase_a(s):
                nxt = step(s, 1)
                before = EC - 1 - SEAM if s.last else EC - 1
                seam = EC - 1 - SEAM if isinstance(s.i, int) and s.c == FULL - 1 else EC - 1
                dve.wait_ge(k_ps, s.c + 1)
                dve.wait_ge(q_ok, s.c + 1)
                dve.tensor_tensor(qk[:, :], q_sb[:, :], E3[:, :], ALU.mult).then_inc(qk_ok, 1)
                if nxt:
                    front_stats_nodes(nxt)
                dve.wait_ge(s_ok, s.c + 1)
                dve.wait_ge(restart_loaded[s.par], 16 * (s.i + 1))
                dve.wait_ge(carried, s.c * 2)
                dve.tensor_tensor_scan(E0[:, :], restart[:, s.par], s_sb[:, :], carry[:, 0:1],
                                       ALU.add, ALU.max).then_inc(max_ok, 1)
                dve.wait_ge(max_ok, s.c + 1)
                dve.tensor_tensor(ga[:, 0:1], restart[:, s.par, 0:1], carry[:, 0:1], ALU.add)
                dve.tensor_tensor(ga[:, 1:EC], restart[:, s.par, 1:EC], E0[:, 0:EC - 1], ALU.add).then_inc(gap0_ok, 1)
                dve.tensor_tensor(gb[:, :], s_sb[:, :], E0[:, :], ALU.subtract)
                dve.wait_ge(gap0_ok, s.c + 1)
                dve.tensor_copy(carry[:, 0:1], E0[:, seam:seam + 1]).then_inc(carried, 1)
                dve.tensor_tensor(ga[:, :], ga[:, :], E0[:, :], ALU.subtract).then_inc(gaps_ok, 1)
                add_rows(s, 0)
                add_rows(s, 1)
                if nxt:
                    front_stats_edges(nxt)
                dve.wait_ge(exp_ok, s.c + 1)
                dve.tensor_tensor_scan(den[:, s.par], ga[:, :], gb[:, :], den[:, 1 - s.par, before:before + 1],
                                       ALU.mult, ALU.add).then_inc(den_ok, 1)
                dve.wait_ge(v_ps, s.c + 1)
                dve.tensor_tensor(bv[:, :], gb[:, :], E4[:, :], ALU.mult).then_inc(bv_ok, 1)
                dve.wait_ge(den_ok, s.c + 1)
                dve.reciprocal(rden[:, :], den[:, s.par]).then_inc(rden_ok, 1)
                dve.wait_ge(bv_ok, s.c + 1)
                dve.tensor_tensor_scan(E2[:, :], ga[:, :], bv[:, :], carry[:, 1:2],
                                       ALU.mult, ALU.add).then_inc(sum_ok, 1)
                dve.wait_ge(sum_ok, s.c + 1)
                dve.tensor_copy(carry[:, 1:2], E2[:, seam:seam + 1]).then_inc(carried, 1)
                dve.tensor_tensor(att[:, :], E2[:, :], rden[:, :], ALU.mult).then_inc(att_ok, 1)
                add_rows(s, 2)
                add_rows(s, 3)
                if nxt:
                    front_rows(nxt, s)
                dve.wait_ge(att_ps, s.c + 1)
                dve.wait_ge(xd_copied, s.c + 1)
                dve.wait_ge(x1_stored[s.par], 16 * s.i)
                dve.tensor_tensor(x1[:, s.par], E1[:, :].rearrange("p (j d) -> p j d", j=ET),
                                  xd_kept[:, s.par], ALU.add).then_inc(x1_ok, 1)

            run(dve, phase_a)

            tilesB = range(NT, NL)

            def frontB_stats(s):
                dve.wait_ge(ys_replaced[s.par], 16 * ET * (s.i + 1))
                dve.wait_ge(yd_loaded[s.par], 16 * (s.i + 1))
                norm_stats(s, tilesB, NT).then_inc(lnB, 1)
                norm_scales(s, 2 * ET, lnB, varB)

            def frontB_rows(s):
                norm_shift(s, 2 * ET, rstdB, shiftB)
                norm_rows(s, tilesB, NT).then_inc(normedB, 1)

            frontB_stats(step(0))
            frontB_rows(step(0))

            def phase_b(s):
                nxt = step(s, 1)
                before = EC - 1 - SEAM if s.last else EC - 1
                if nxt:
                    frontB_stats(nxt)
                dve.wait_ge(m_ps, s.c + 1)
                dve.wait_ge(ew_loaded[s.par], 16 * (s.i + 1))
                dve.scalar_tensor_tensor(msg[:, :], ew[:, s.par], cols[:, 2:3], E2[:, :],
                                         ALU.mult, ALU.add).then_inc(msg_ok, 1)
                dve.wait_ge(msg_ok, s.c + 1)
                dve.wait_ge(restartB_loaded[s.par], 16 * (s.i + 1))
                dve.wait_ge(g_ps, s.c)
                dve.tensor_tensor_scan(top[:, s.par], restart[:, s.par], msg[:, :], top[:, 1 - s.par, before:before + 1],
                                       ALU.add, ALU.max).then_inc(top_ok, 1)
                if nxt:
                    frontB_rows(nxt)
                dve.wait_ge(r_ps, s.c + 1)
                dve.wait_ge(out_put[s.par], 16 * ET * s.i)
                dve.tensor_tensor(x1[:, s.par], E4[:, :].rearrange("p (j d) -> p j d", j=ET),
                                  xd[:, s.par], ALU.add).then_inc(row_ok, 1)

            run(dve, phase_b)

        @block.scalar
        def _(act):
            def turned(dst_tile, src_bank, func=ACT.Relu):
                return act.activation(dst_tile[:, :].rearrange("f (p j) -> f j p", j=ET),
                                      src_bank[:, :].rearrange("f (j p) -> f j p", j=ET), func)

            def normalise(s, now=None):
                act.wait_ge(shift_ready, s.c + 1)
                if now:
                    act.wait_ge(hT_ps, DT * now.c)
                for t in range(ACT_TILES):
                    ins = act.activation(h[:, s.par, t], x_in[:, s.par, t], ACT.Relu,
                                         bias=shift[:, t:t + 1], scale=rstd[:, t:t + 1])
                ins.then_inc(normed_act, 1)

            def keep_xd(s):
                act.wait_ge(xd_got[s.par], 16 * ET * (s.i + 1))
                act.activation(xd_kept[:, s.par], xd[:, s.par], ACT.Copy).then_inc(xd_copied, 1)

            normalise(step(0))
            keep_xd(step(0))

            def phase_a(s):
                nxt = step(s, 1)

                def evac_h(k):
                    n = DT * s.c + k
                    act.wait_ge(hT_ps, n + 1)
                    act.wait_ge(hid_ps, n - 1 if k else n)
                    act.activation(hT[:, k % 2], T_ps[:, :], ACT.Relu).then_inc(hT_ok, 1)

                def evac_hid(k):
                    n = DT * s.c + k
                    act.wait_ge(hid_ps, n + 1)
                    act.wait_ge(o_ps, n - 1 if k else n)
                    act.activation(hid[:, k % 2], H_ps[:, :], ACT.Relu, bias=cols[:, 1:2]).then_inc(hid_ok, 1)

                act.wait_ge(hsT_ps, s.c + 1)
                act.wait_ge(v_ps, s.c)
                turned(hsT, E0).then_inc(hsT_ok, 1)
                act.wait_ge(hdT_ps, s.c + 1)
                turned(hdT, E1).then_inc(hdT_ok, 1)
                act.wait_ge(attrT_ps, s.c + 1)
                act.wait_ge(s_ps, s.c)
                act.activation(attrT[:, :], E4[:, 0:P], ACT.Copy).then_inc(attrT_ok, 1)
                evac_h(0)
                act.wait_ge(q_ps, s.c + 1)
                act.wait_ge(qk_ok, s.c)
                act.activation(q_sb[:, :], E2[:, :], ACT.Copy).then_inc(q_ok, 1)
                evac_h(1)
                evac_hid(0)
                act.wait_ge(s_ps, s.c + 1)
                act.wait_ge(gaps_ok, s.c)
                act.activation(s_sb[:, :], E0[:, :], ACT.Copy).then_inc(s_ok, 1)
                evac_h(2)
                evac_hid(1)
                act.wait_ge(gaps_ok, s.c + 1)
                act.activation(ga[:, :], ga[:, :], ACT.Exp)
                act.activation(gb[:, :], gb[:, :], ACT.Exp).then_inc(exp_ok, 1)
                evac_h(3)
                evac_hid(2)
                evac_hid(3)
                if nxt:
                    keep_xd(nxt)
                    normalise(nxt, s)

            run(act, phase_a)

            def phase_b(s):
                act.wait_ge(ysT_ps, s.c + 1)
                turned(hsT, E0).then_inc(ysT_ok, 1)
                act.wait_ge(ydT_ps, s.c + 1)
                act.wait_ge(g_ps, s.c)
                turned(hdT, E1).then_inc(ydT_ok, 1)
                act.wait_ge(g_ps, s.c + 1)
                act.activation(hidB[:, :], E3[:, :], ACT.Relu, bias=cols[:, 3:4]).then_inc(g_ok, 1)

            run(act, phase_b)

        @block.tensor
        def _(pe):
            pe.wait_ge(consts_pool, 6)
            pe.wait_ge(w_in, 16 * 16)
            for n in range(4):
                pe.transpose(E0[:, n * P:(n + 1) * P], wload[:, n], ident[:, :])
            pe.transpose(E1[:, 0:P], we_rows[:, :, :].rearrange("p j k -> p (j k)"), ident[:, :]).then_inc(setup_ps, 1)
            pe.wait_ge(setup_sb, 1)
            pe.wait_ge(col_in, 3 * 16)
            pe.matmul(E2[:, 0:P], WdT[:, :], W1b[:, :], start=True, stop=True)
            pe.matmul(E3[:, 0:1], W1b[:, :], cols[:, 0:1], start=True, stop=True).then_inc(setup_ps, 1)
            pe.wait_ge(setup_sb, 2)
            pe.wait_ge(b2_split, 11)

            def turn(bank_, s, first):
                for j in range(ET):
                    ins = pe.transpose(bank_[:, j * P:(j + 1) * P], h[:, s.par, first + j], ident[:, :])
                return ins

            def rows_out(bank_, hidden):
                pe.matmul(bank_[:, :], ones_bf[:, :], b2_rows[:, :], start=True, stop=False, skip_group_check=True)
                for j in range(ET):
                    ins = pe.matmul(bank_[:, j * P:(j + 1) * P], hidden(j), W2s[:, :],
                                    start=False, stop=True, skip_group_check=True)
                return ins

            def phase_a(s):
                def turn_h(k):
                    pe.wait_ge(hT_ok, DT * s.c + k)
                    turn(T_ps, s, ET * k).then_inc(hT_ps, 1)

                def hidden(k):
                    n = DT * s.c + k
                    pe.wait_ge(hT_ok, n + 1)
                    pe.wait_ge(hid_ok, n)
                    pe.matmul(H_ps[:, :], W1a[:, :], hT[:, k % 2], start=True, stop=True).then_inc(hid_ps, 1)

                def second(k):
                    n = DT * s.c + k
                    pe.wait_ge(hid_ok, n + 1)
                    pe.wait_ge(out_ok, n)
                    rows_out(O_ps, lambda j: hid[:, k % 2, j * P:(j + 1) * P]).then_inc(o_ps, 1)

                pe.wait_ge(normed_dve, s.c + 1)
                pe.wait_ge(normed_act, s.c + 1)
                pe.wait_ge(gaps_ok, s.c)
                turn(E0, s, NT).then_inc(hsT_ps, 1)
                turn_h(0)
                pe.wait_ge(x1_ok, s.c)
                turn(E1, s, NT + ET).then_inc(hdT_ps, 1)
                pe.wait_ge(attr_loaded[s.par], 16 * (s.i + 1))
                pe.wait_ge(bv_ok, s.c)
                pe.transpose(E4[:, 0:P], attr[:, s.par].rearrange("p j k -> p (j k)"), ident[:, :]).then_inc(attrT_ps, 1)
                pe.wait_ge(hdT_ok, s.c + 1)
                pe.wait_ge(att_ok, s.c)
                pe.matmul(E2[:, :], WqT[:, :], hdT[:, :], start=True, stop=True).then_inc(q_ps, 1)
                pe.wait_ge(hsT_ok, s.c + 1)
                pe.matmul(E3[:, :], WkT[:, :], hsT[:, :], start=True, stop=True).then_inc(k_ps, 1)
                pe.wait_ge(attrT_ok, s.c + 1)
                pe.matmul(E4[:, :], WvT[:, :], hsT[:, :], start=True, stop=True).then_inc(v_ps, 1)
                turn_h(1)
                hidden(0)
                pe.wait_ge(qk_ok, s.c + 1)
                pe.matmul(E0[:, :], head_sum[:, :], qk[:, :], start=True, stop=False, skip_group_check=True)
                for j in range(ET):
                    ins = pe.matmul(E0[:, j::ET], WeT[:, j], attrT[:, :], start=False, stop=True, skip_group_check=True)
                ins.then_inc(s_ps, 1)
                turn_h(2)
                hidden(1)
                second(0)
                turn_h(3)
                hidden(2)
                second(1)
                hidden(3)
                second(2)
                second(3)
                pe.wait_ge(att_ok, s.c + 1)
                for j in range(ET):
                    ins = pe.transpose(E1[:, j * P:(j + 1) * P], att[:, j::ET], ident[:, :])
                ins.then_inc(att_ps, 1)

            run(pe, phase_a)

            pe.wait_ge(x1_ok, STEPS)
            pe.wait_ge(bv_ok, STEPS)

            def phase_b(s):
                pe.wait_ge(normedB, s.c + 1)
                pe.wait_ge(ysT_ok, s.c)
                turn(E0, s, NT).then_inc(ysT_ps, 1)
                turn(E1, s, NT + ET).then_inc(ydT_ps, 1)
                pe.wait_ge(ysT_ok, s.c + 1)
                pe.wait_ge(msg_ok, s.c)
                pe.matmul(E2[:, :], Ws[:, :], hsT[:, :], start=True, stop=True).then_inc(m_ps, 1)
                pe.wait_ge(ydT_ok, s.c + 1)
                pe.wait_ge(g_ok, s.c)
                pe.matmul(E3[:, :], Wh[:, :], hdT[:, :], start=True, stop=False)
                pe.wait_ge(top_ok, s.c + 1)
                pe.matmul(E3[:, :], W1b[:, :], top[:, s.par], start=False, stop=True).then_inc(g_ps, 1)
                pe.wait_ge(g_ok, s.c + 1)
                pe.wait_ge(row_ok, s.c)
                rows_out(E4, lambda j: hidB[:, j::ET]).then_inc(r_ps, 1)

            run(pe, phase_b)


_INS = ["x", "src", "dst", "edge_attr_32", "edge_weight", "L0_gnn_Wq", "L0_gnn_Wk", "L0_gnn_Wv", "L0_gnn_We",
        "L1_gnn_Wm", "L1_gnn_bm", "L1_gnn_W1", "L1_gnn_b1", "L1_gnn_W2", "L1_gnn_b2"]


def kernel(**inputs):
    import concourse.bacc as bacc
    from concourse.bass_utils import run_bass_kernel_spmd

    nc = bacc.Bacc("TRN2", target_bir_lowering=False, num_devices=1)
    arrays, args = {}, []
    for name in _INS:
        a = np.ascontiguousarray(inputs[name])
        arrays[f"in_{name}"] = a
        args.append(nc.dram_tensor(f"in_{name}", a.shape, mybir.dt.from_np(a.dtype), kind="ExternalInput").ap())
    shape = inputs["x"].shape
    args.append(nc.dram_tensor("out_x", shape, F32, kind="ExternalOutput").ap())
    gnn_two_layers(nc, *args)
    return run_bass_kernel_spmd(nc, [arrays], core_ids=[0]).results[0]["out_x"]
```

```python
from contextlib import ExitStack

import numpy as np

import concourse.bass as bass
from concourse import mybir

F32 = mybir.dt.float32
BF16 = mybir.dt.bfloat16
I32 = mybir.dt.int32
U32 = mybir.dt.uint32
ALU = mybir.AluOpType
ACT = mybir.ActivationFunctionType

P = 128
D = 128
HEADS = 8
CH = D // HEADS
KA = 32
ET = 4
EC = ET * P
NT = 16
NCH = NT * P
DT = NT // ET
NL = NT + 2 * ET
ACT_TILES = 20
ROOT_STEPS = 3
ROOT_BITS = 0x5F3759DF
EPS = 1e-5
NEG = -3.0e38
NO_ROW = 1 << 20


class Step:

    def __init__(self, i, par, last, n_edges, n_nodes):
        self.i, self.par, self.last = i, par, last
        self.c = i * 2 + par
        self.edge0 = n_edges - EC if last else i * (2 * EC) + par * EC
        self.node0 = n_nodes - NCH if last else i * (2 * NCH) + par * NCH

    def edges(self):
        return bass.ds(self.edge0, EC)

    def nodes(self):
        return bass.ds(self.node0, NCH)


def gnn_two_layers(nc, x, src, dst, edge_attr, edge_weight, Wq, Wk, Wv, We, Wm, bm, W1, b1, W2, b2, out):
    N, E = x.shape[0], src.shape[0]
    STEPS = -(-E // EC)
    assert STEPS == -(-N // NCH) and STEPS % 2 == 1
    FULL = STEPS - 1
    LOOPS = (FULL - 2) // 2
    LOOPS_B = LOOPS - 1
    EPP = E // 125

    def step(c, k=0):
        if isinstance(c, Step):
            if isinstance(c.i, int):
                return step(c.c + k)
            p = c.par + k
            return Step(c.i + p // 2, p % 2, False, E, N)
        n = c + k
        return Step(n // 2, n % 2, n == FULL, E, N) if n <= FULL else None

    def run(eng, body, rounds=LOOPS):
        for c in range(2):
            body(step(c))
        with eng.Fori(1, rounds) as i:
            for par in range(2):
                body(Step(i, par, False, E, N))
        for c in range(2 * rounds, STEPS):
            body(step(c))

    with ExitStack() as ctx:
        def sb(name, shape, dt=F32):
            return ctx.enter_context(nc.sbuf_tensor(name, shape, dt))

        def sem(name):
            return ctx.enter_context(nc.semaphore(name))

        def sem2(name):
            return [sem(f"{name}_{p}") for p in range(2)]

        bank = [ctx.enter_context(nc.psum_tensor(f"bank{b}", [P, 512], F32)) for b in range(8)]
        T_ps, H_ps, O_ps, E0, E1, E2, E3, E4 = bank

        restart_row = nc.dram_tensor("restart_row", [E], F32).ap()
        last_edge = nc.dram_tensor("last_edge", [N, 1], I32).ap()
        xs_rows = nc.dram_tensor("xs_rows", [E, D], F32).ap()
        x1_rows = nc.dram_tensor("x1_rows", [E, D], F32).ap()

        ident = sb("ident", [P, P])
        head_sum = sb("head_sum", [P, P])
        wload = sb("wload", [P, 4, P])
        we_rows = sb("we_rows", [P, ET, KA])
        WqT, WkT, WvT, WdT = (sb(n, [P, P]) for n in ("WqT", "WkT", "WvT", "WdT"))
        WeT = sb("WeT", [P, ET, P])
        Ws = sb("Ws", [P, P])
        W1a, W1b, W2s, Wh = (sb(n, [P, P]) for n in ("W1a", "W1b", "W2s", "Wh"))
        cols = sb("cols", [P, 4])
        b2_rep = sb("b2_rep", [P, 512])
        b2_part = sb("b2_part", [P, 3, 512], BF16)
        b2_rest = sb("b2_rest", [P, 2, 512])
        b2_rows = sb("b2_rows", [P, 512], BF16)
        ones_bf = sb("ones_bf", [P, P], BF16)

        src_i = sb("src_i", [P, STEPS, ET], I32)
        dst_i = sb("dst_i", [P, STEPS, ET], I32)
        next_i = sb("next_i", [P, STEPS, ET], I32)
        inner = sb("inner", [P, STEPS, ET])
        end_i = sb("end_i", [P, STEPS, ET], I32)
        edge_i = sb("edge_i", [P, STEPS, ET], I32)
        found = sb("found", [P, STEPS, ET], I32)
        dst_l = sb("dst_l", [125, EPP], I32)
        prev_l = sb("prev_l", [125, EPP], I32)
        restart_l = sb("restart_l", [125, EPP])
        no_rows = sb("no_rows", [125, N // 125], I32)
        gather_ix = sb("gather_ix", [P, 2, 2, ET], I32)
        table_ix = sb("table_ix", [P, 2, 2, 2 * ET], I32)
        table_got = sb("table_got", [P, 2, 2 * ET], I32)

        x_in = sb("x_in", [P, 2, NT, D])
        x_out = sb("x_out", [P, 2, NT, D])
        h = sb("h", [P, 2, NL, D])
        xs = sb("xs", [P, 2, ET, D])
        xd = sb("xd", [P, 2, ET, D])
        xd_kept = sb("xd_kept", [P, 2, ET, D])
        x1 = sb("x1", [P, 2, ET, D])
        attr = sb("attr", [P, 2, ET, KA])
        restart = sb("restart", [P, 2, EC])
        ew = sb("ew", [P, 2, EC])
        stats = sb("stats", [P, NL, 6])
        sums, diff, q4, sq, var, guess, root, root_t, root_u = (sb(n, [P, NL]) for n in (
            "sums", "diff", "q4", "sq", "var", "guess", "root", "root_t", "root_u"))
        rstd, shift = sb("rstd", [P, 2, NL]), sb("shift", [P, 2, NL])
        hsT, hdT = sb("hsT", [P, 2, EC]), sb("hdT", [P, 2, EC])
        q_sb, qk, s_sb = (sb(n, [P, EC]) for n in ("q_sb", "qk", "s_sb"))
        attrT = sb("attrT", [P, P])
        ga, gb, bv = (sb(n, [P, EC]) for n in ("ga", "gb", "bv"))
        den, acc = sb("den", [P, 2, EC]), sb("acc", [P, 2, EC])
        rden = sb("rden", [P, ET, HEADS])
        carry = sb("carry", [P, 1])
        hT = sb("hT", [P, 2, 512])
        hid = sb("hid", [P, 2, 512])
        msg = sb("msg", [P, EC])
        top = sb("top", [P, 2, EC])
        hidB = sb("hidB", [P, EC])

        w_in, col_in, b2_in, ix_in, l_in, ew_in0 = (sem(n) for n in
                                                    ("w_in", "col_in", "b2_in", "ix_in", "l_in", "ew_in0"))
        consts_pool, consts_dve = sem("consts_pool"), sem("consts_dve")
        setup_ps, setup_sb = sem("setup_ps"), sem("setup_sb")
        b2_split = sem("b2_split")
        restart_ready, restart_stored = sem("restart_ready"), sem("restart_stored")
        ends_ready, table_cleared = sem("ends_ready"), sem("table_cleared")
        no_rows_ready, ends_found = sem("no_rows_ready"), sem("ends_found")
        x_loaded = [sem2(f"x_loaded_{half}") for half in range(2)]
        attr_loaded, restart_loaded = sem2("attr_loaded"), sem2("restart_loaded")
        xs_got, xd_got = sem2("xs_got"), sem2("xd_got")
        xs_stored, x1_stored, out_stored = sem2("xs_stored"), sem2("x1_stored"), sem2("out_stored")
        table_put, table_read = sem2("table_put"), sem2("table_read")
        ys_loaded, yd_loaded, ew_loaded, restartB_loaded = (sem2(n) for n in
                                                            ("ys_loaded", "yd_loaded", "ew_loaded", "restartB_loaded"))
        ys_replaced, out_put = sem2("ys_replaced"), sem2("out_put")
        gate, sp_gate = sem("gate"), sem("sp_gate")
        ix_staged, table_staged, found_kept = sem("ix_staged"), sem("table_staged"), sem("found_kept")
        ln = sem("ln")
        half_ok, root_ok = sem("half_ok"), sem("root_ok")
        scales_ready = sem("scales_ready")
        nodes_normed, edges_normed, edges_normed_act = sem("nodes_normed"), sem("edges_normed"), sem("edges_normed_act")
        xd_copied = sem("xd_copied")
        hsT_ps, hdT_ps, attrT_ps, q_ps, k_ps, v_ps, s_ps, acc_ps, den_ps = (sem(n) for n in
            ("hsT_ps", "hdT_ps", "attrT_ps", "q_ps", "k_ps", "v_ps", "s_ps", "acc_ps", "den_ps"))
        hsT_ok, hdT_ok, attrT_ok, q_ok, s_ok = (sem(n) for n in ("hsT_ok", "hdT_ok", "attrT_ok", "q_ok", "s_ok"))
        hT_ps, hid_ps, o_ps, hT_ok, hid_ok, out_ok = (sem(n) for n in
            ("hT_ps", "hid_ps", "o_ps", "hT_ok", "hid_ok", "out_ok"))
        qk_ok, max_ok, gap0_ok, gaps_ok, carried = (sem(n) for n in ("qk_ok", "max_ok", "gap0_ok", "gaps_ok", "carried"))
        exp_ok, den_ok, bv_ok, acc_ok, rden_ok, att_ok, x1_ok = (sem(n) for n in
            ("exp_ok", "den_ok", "bv_ok", "acc_ok", "rden_ok", "att_ok", "x1_ok"))
        phaseA_stored = sem("phaseA_stored")
        lnB, scalesB, normedB, ydB_kept = (sem(n) for n in ("lnB", "scalesB", "normedB", "ydB_kept"))
        ysT_ps, ydT_ps, m_ps, g_ps, r_ps = (sem(n) for n in ("ysT_ps", "ydT_ps", "m_ps", "g_ps", "r_ps"))
        ysT_ok, ydT_ok, msg_ok, top_ok, g_ok, row_ok = (sem(n) for n in
            ("ysT_ok", "ydT_ok", "msg_ok", "top_ok", "g_ok", "row_ok"))
        ixB_staged, endB_staged = sem("ixB_staged"), sem("endB_staged")

        attr_v = lambda s: edge_attr[s.edges(), :].rearrange("(p j) k -> p j k", j=ET)
        rows_v = lambda t, s: t[s.edges(), :].rearrange("(p j) d -> p j d", j=ET)
        nodes_v = lambda t, s: t[s.nodes(), :].rearrange("(p j) d -> p j d", j=NT)
        spread = lambda t, s: t[s.edges()].partition_broadcast(P)

        block = ctx.enter_context(nc.Block())

        @block.sync
        def _(sp):
            def load_node_rows(s, half):
                t = slice(half * NT // 2, (half + 1) * NT // 2)
                sp.dma_start(x_in[:, s.par, t], nodes_v(x, s)[:, t]).then_inc(x_loaded[half][s.par], 16)

            def load_attr(s):
                sp.dma_start(attr[:, s.par], attr_v(s)).then_inc(attr_loaded[s.par], 16)

            def load_restart(s, done):
                sp.dma_start(restart[:, s.par], spread(restart_row, s)).then_inc(done[s.par], 16)

            full = FULL * EC
            for tile_, a in ((src_i, src), (dst_i, dst)):
                sp.dma_start(tile_[:, 0:FULL, :], a[0:full].rearrange("(c p j) -> p c j", p=P, j=ET)).then_inc(ix_in, 16)
                sp.dma_start(tile_[:, FULL, :], a[E - EC:E].rearrange("(p j) -> p j", j=ET)).then_inc(ix_in, 16)
            sp.dma_start(dst_l[:, :], dst.rearrange("(p j) -> p j", p=125)).then_inc(l_in, 16)
            sp.wait_ge(consts_pool, 1)
            sp.dma_start(prev_l[0:1, 1:EPP], dst[0:EPP - 1].rearrange("(a j) -> a j", a=1)).then_inc(l_in, 16)
            sp.dma_start(prev_l[1:125, :], dst[EPP - 1:E - 1].rearrange("(p j) -> p j", j=EPP)).then_inc(l_in, 16)
            sp.dma_start(next_i[:, 0:FULL, :], dst[1:full + 1].rearrange("(c p j) -> p c j", p=P, j=ET)).then_inc(ix_in, 16)
            sp.dma_start(next_i[0:P - 1, FULL, :], dst[E - EC + 1:E - ET + 1].rearrange("(p j) -> p j", j=ET)).then_inc(ix_in, 16)
            sp.dma_start(next_i[P - 1:P, FULL, 0:ET - 1], dst[E - ET + 1:E].rearrange("(a j) -> a j", a=1)).then_inc(ix_in, 16)
            for c in range(2):
                for half in range(2):
                    load_node_rows(step(c), half)
                load_attr(step(c))
            for n, w in enumerate((Wq, Wk, Wv, Wm[0:D, :])):
                sp.dma_start(wload[:, n], w[:, :]).then_inc(w_in, 16)
            for hd in range(HEADS):
                sp.dma_start(we_rows[CH * hd:CH * (hd + 1)],
                             We[hd:hd + 1, :].unsqueeze(0).broadcast_to([CH, ET, KA])).then_inc(w_in, 16)
            sp.dma_start(Ws[:, :], Wm[D:2 * D, :]).then_inc(w_in, 16)
            sp.dma_start(W1a[:, :], W1[0:D, :]).then_inc(w_in, 16)
            sp.dma_start(W1b[:, :], W1[D:2 * D, :]).then_inc(w_in, 16)
            sp.dma_start(W2s[:, :], W2[:, :]).then_inc(w_in, 16)
            for n, v in enumerate((bm, b1, Wm[2 * D])):
                sp.dma_start(cols[:, n:n + 1], v.rearrange("(p a) -> p a", a=1)).then_inc(col_in, 16)
            sp.dma_start(b2_rep[:, 0:D], b2.partition_broadcast(P)).then_inc(b2_in, 16)
            sp.wait_ge(restart_ready, 1)
            sp.dma_start(restart_row.rearrange("(p j) -> p j", p=125), restart_l[:, :]).then_inc(restart_stored, 16)
            sp.wait_ge(no_rows_ready, 1)
            sp.dma_start(last_edge.rearrange("(p j) a -> p (j a)", p=125), no_rows[:, :]).then_inc(table_cleared, 16)
            sp.wait_ge(restart_stored, 16)
            for c in range(2):
                load_restart(step(c), restart_loaded)

            def open_gate():
                sp.sem_inc(sp_gate, 1)

            def store_xs(s):
                if s.last:
                    sp.wait_ge(xs_stored[1 - s.par], 16 * s.i)
                sp.wait_ge(xs_got[s.par], 16 * ET * (s.i + 1))
                open_gate()
                sp.dma_start(rows_v(xs_rows, s), xs[:, s.par]).then_inc(xs_stored[s.par], 16)

            store_xs(step(0))
            store_xs(step(1))

            def phase_a(s):
                far = step(s, 2)
                if far:
                    store_xs(far)
                    sp.wait_ge(attrT_ps, s.c + 1)
                    open_gate()
                    load_attr(far)
                    sp.wait_ge(gaps_ok, s.c + 1)
                    open_gate()
                    load_restart(far, restart_loaded)
                if far:
                    sp.wait_ge(out_ok, DT * s.c + 2)
                    open_gate()
                    load_node_rows(far, 0)
                if s.last:
                    sp.wait_ge(out_stored[1 - s.par], 16 * s.i)
                sp.wait_ge(out_ok, DT * (s.c + 1))
                open_gate()
                if far:
                    load_node_rows(far, 1)
                sp.dma_start(nodes_v(out, s), x_out[:, s.par]).then_inc(out_stored[s.par], 16)
                if s.last:
                    sp.wait_ge(x1_stored[1 - s.par], 16 * s.i)
                sp.wait_ge(x1_ok, s.c + 1)
                open_gate()
                sp.dma_start(rows_v(x1_rows, s), x1[:, s.par]).then_inc(x1_stored[s.par], 16)

            run(sp, phase_a)

            for p in range(2):
                uses = FULL // 2 + (1 - p)
                for stored in (xs_stored, x1_stored, out_stored):
                    sp.wait_ge(stored[p], 16 * uses)
            sp.sem_inc(phaseA_stored, 1)

            def load_ys(s):
                sp.dma_start(xs[:, s.par], rows_v(xs_rows, s)).then_inc(ys_loaded[s.par], 16)

            def load_yd(s):
                sp.dma_start(xd[:, s.par], rows_v(x1_rows, s)).then_inc(yd_loaded[s.par], 16)

            def load_ew(s):
                sp.dma_start(ew[:, s.par], spread(edge_weight, s)).then_inc(ew_loaded[s.par], 16)

            for c in range(2):
                load_ys(step(c))
                load_yd(step(c))
                load_ew(step(c))
                load_restart(step(c), restartB_loaded)
            sp.wait_ge(normedB, 1)
            load_ys(step(2))
            sp.wait_ge(ydB_kept, 1)
            load_yd(step(2))

            def phase_b(s):
                far, farther = step(s, 2), step(s, 3)
                if farther:
                    sp.wait_ge(normedB, s.c + 2)
                    open_gate()
                    load_ys(farther)
                    sp.wait_ge(ydB_kept, s.c + 2)
                    open_gate()
                    load_yd(farther)
                if far:
                    sp.wait_ge(msg_ok, s.c + 1)
                    open_gate()
                    load_ew(far)
                    sp.wait_ge(top_ok, s.c + 1)
                    open_gate()
                    load_restart(far, restartB_loaded)

            run(sp, phase_b, LOOPS_B)
            for p in range(2):
                uses = FULL // 2 + (1 - p)
                sp.wait_ge(out_put[p], 16 * ET * uses)

        @block.gpsimd
        def _(pool):
            pool.memset(prev_l[:, :], -1)
            pool.memset(next_i[:, :, :], -1).then_inc(consts_pool, 1)
            pool.memset(no_rows[:, :], NO_ROW).then_inc(no_rows_ready, 1)
            pool.memset(ident[:, :], 0.0)
            pool.memset(head_sum[:, :], 1.0).then_inc(consts_pool, 1)
            pool.iota(edge_i[:, 0:FULL, :], pattern=[[EC, FULL], [1, ET]], base=0, channel_multiplier=ET)
            pool.iota(edge_i[:, FULL, :], pattern=[[1, ET]], base=E - EC, channel_multiplier=ET).then_inc(consts_pool, 1)
            pool.wait_ge(consts_pool, 3)
            pool.affine_select(out=ident[:, :], in_=ident[:, :], compare_op=ALU.not_equal, fill=1.0,
                               base=0, pattern=[[-1, P]], channel_multiplier=1).then_inc(consts_pool, 1)
            blocks = head_sum[:, :].rearrange("p (g r) -> p g r", r=CH)
            pool.affine_select(out=blocks, in_=blocks, compare_op=ALU.is_ge, fill=0.0, base=0,
                               pattern=[[-CH, HEADS], [0, CH]], channel_multiplier=1).then_inc(consts_pool, 1)
            pool.wait_ge(consts_pool, 5)
            pool.affine_select(out=blocks, in_=blocks, compare_op=ALU.is_ge, fill=0.0, base=CH - 1,
                               pattern=[[CH, HEADS], [0, CH]], channel_multiplier=-1).then_inc(consts_pool, 1)

            def open_gate():
                pool.sem_inc(gate, 1)

            def gather(s, first):
                pool.wait_ge(xs_got[s.par], 16 * ET * s.i)
                pool.wait_ge(xd_got[s.par], 16 * ET * s.i)
                open_gate()
                pool.tensor_copy(gather_ix[:, s.par, 0], src_i[:, bass.ds(s.c, 1), :].rearrange("p a j -> p (a j)"))
                pool.tensor_copy(gather_ix[:, s.par, 1],
                                 dst_i[:, bass.ds(s.c, 1), :].rearrange("p a j -> p (a j)")).then_inc(ix_staged, 1)
                pool.wait_ge(ix_staged, s.c + 1)
                if not first:
                    pool.wait_ge(edges_normed, s.c - 1)
                    pool.wait_ge(edges_normed_act, s.c - 1)
                    pool.wait_ge(xd_copied, s.c - 1)
                    pool.wait_ge(xs_stored[s.par], 16 * s.i)
                open_gate()
                for rows, which, got in ((xs, 0, xs_got), (xd, 1, xd_got)):
                    for j in range(ET):
                        pool.indirect_dma_start(
                            out=rows[:, s.par, j], out_offset=None, in_=x,
                            in_offset=bass.IndirectOffsetOnAxis(ap=gather_ix[:, s.par, which, j:j + 1].bitcast(U32), axis=0),
                        ).then_inc(got[s.par], 16)

            pool.wait_ge(ix_in, 7 * 16)
            gather(step(0), True)
            gather(step(1), True)
            gather(step(2), False)

            def table_columns(a, first, width):
                return a[:, bass.ds(first, width), :].rearrange("p a j -> p (a j)")

            def put_entries(k, uses, n, first, width):
                cols_ = width * ET
                pool.wait_ge(table_put[k], 16 * uses)
                open_gate()
                pool.tensor_copy(table_ix[:, k, 0, 0:cols_], table_columns(end_i, first, width))
                pool.tensor_copy(table_ix[:, k, 1, 0:cols_], table_columns(edge_i, first, width)).then_inc(table_staged, 1)
                pool.wait_ge(table_staged, n + 1)
                open_gate()
                for j in range(cols_):
                    pool.indirect_dma_start(
                        out=last_edge, out_offset=bass.IndirectOffsetOnAxis(
                            ap=table_ix[:, k, 0, j:j + 1].bitcast(U32), axis=0),
                        in_=table_ix[:, k, 1, j:j + 1], in_offset=None,
                        bounds_check=N - 1, oob_is_err=False).then_inc(table_put[k], 16)

            def read_entries(k, uses, n, first, width):
                cols_ = width * ET
                pool.wait_ge(table_read[k], 16 * uses)
                open_gate()
                pool.tensor_copy(table_ix[:, k, 0, 0:cols_], table_columns(src_i, first, width)).then_inc(table_staged, 1)
                pool.wait_ge(table_staged, n + 1)
                open_gate()
                for j in range(cols_):
                    pool.indirect_dma_start(
                        out=table_got[:, k, j:j + 1], out_offset=None, in_=last_edge,
                        in_offset=bass.IndirectOffsetOnAxis(ap=table_ix[:, k, 0, j:j + 1].bitcast(U32), axis=0),
                    ).then_inc(table_read[k], 16)

            def keep_entries(k, uses, first, width):
                cols_ = width * ET
                pool.wait_ge(table_read[k], 16 * uses)
                open_gate()
                pool.tensor_copy(table_columns(found, first, width), table_got[:, k, 0:cols_]).then_inc(found_kept, 1)

            def phase_a(s, table_work):
                farther = step(s, 3)
                if farther:
                    gather(farther, False)
                table_work(s)

            HALF = LOOPS // 2 + 1
            put_steps = 2 * HALF

            pool.wait_ge(ends_ready, 2)
            pool.wait_ge(table_cleared, 16)

            def put_work(s):
                put_entries(s.par, 2 * ET * s.i, s.c, s.c * 2, 2)

            for c in range(2):
                phase_a(step(c), put_work)
            with pool.Fori(1, HALF) as i:
                for par in range(2):
                    phase_a(Step(i, par, False, E, N), put_work)
            left = STEPS - 2 * put_steps
            assert left == 1
            for p in range(2):
                pool.wait_ge(table_put[p], 16 * 2 * ET * HALF)
            put_entries(0, 2 * ET * HALF, put_steps, FULL, 1)
            pool.wait_ge(table_put[0], 16 * (2 * ET * HALF + ET))

            def read_work(s, base=put_steps):
                n = s.c - base
                read_entries(s.par, 2 * ET * (s.i - HALF), s.c + 1, n * 2, 2)
                keep_entries(s.par, 2 * ET * (s.i - HALF + 1), n * 2, 2)

            with pool.Fori(HALF, LOOPS) as i:
                for par in range(2):
                    phase_a(Step(i, par, False, E, N), read_work)
            for c in range(2 * LOOPS, STEPS):
                phase_a(step(c), lambda s: read_work(s) if 2 * (s.c - put_steps) < FULL else None)
            done = min(STEPS, put_steps + FULL // 2) - put_steps
            reads = [sum(1 for n in range(done) if (n + put_steps) % 2 == p) for p in range(2)]
            staged = put_steps + 1 + done
            first = 2 * done
            while first < STEPS:
                width = min(2, STEPS - first)
                k = (done + put_steps) % 2
                read_entries(k, 2 * ET * reads[k], staged, first, width)
                keep_entries(k, 2 * ET * reads[k] + width * ET, first, width)
                reads[k] += 1
                staged, done, first = staged + 1, done + 1, first + width

            def replace_rows(s):
                pool.wait_ge(ys_replaced[s.par], 16 * ET * s.i)
                open_gate()
                pool.tensor_copy(gather_ix[:, s.par, 0],
                                 found[:, bass.ds(s.c, 1), :].rearrange("p a j -> p (a j)")).then_inc(ixB_staged, 1)
                pool.wait_ge(ixB_staged, s.c + 1)
                pool.wait_ge(ys_loaded[s.par], 16 * (s.i + 1))
                open_gate()
                for j in range(ET):
                    pool.indirect_dma_start(
                        out=xs[:, s.par, j], out_offset=None, in_=x1_rows,
                        in_offset=bass.IndirectOffsetOnAxis(ap=gather_ix[:, s.par, 0, j:j + 1].bitcast(U32), axis=0),
                        bounds_check=E - 1, oob_is_err=False).then_inc(ys_replaced[s.par], 16)

            def put_rows(s):
                pool.wait_ge(out_put[s.par], 16 * ET * s.i)
                open_gate()
                pool.tensor_copy(gather_ix[:, s.par, 1],
                                 end_i[:, bass.ds(s.c, 1), :].rearrange("p a j -> p (a j)")).then_inc(endB_staged, 1)
                pool.wait_ge(endB_staged, s.c + 1)
                pool.wait_ge(row_ok, s.c + 1)
                if s.last:
                    pool.wait_ge(out_put[1 - s.par], 16 * ET * s.i)
                open_gate()
                for j in range(ET):
                    pool.indirect_dma_start(
                        out=out, out_offset=bass.IndirectOffsetOnAxis(
                            ap=gather_ix[:, s.par, 1, j:j + 1].bitcast(U32), axis=0),
                        in_=x1[:, s.par, j], in_offset=None,
                        bounds_check=N - 1, oob_is_err=False).then_inc(out_put[s.par], 16)

            pool.wait_ge(phaseA_stored, 1)
            pool.wait_ge(found_kept, done)
            open_gate()
            for c in range(3):
                replace_rows(step(c))

            def phase_b(s):
                farther = step(s, 3)
                if farther:
                    replace_rows(farther)
                put_rows(s)

            run(pool, phase_b, LOOPS_B)

        @block.vector
        def _(dve):
            def row_of(s, t):
                return (x_in[:, s.par, t] if t < NT else xs[:, s.par, t - NT] if t < NT + ET
                        else xd[:, s.par, t - NT - ET])

            dve.memset(ones_bf[:, :], 1.0)
            dve.memset(b2_rows[:, :], 0.0)
            dve.memset(carry[:, :], 0.0)
            dve.memset(den[:, :, :], 0.0)
            dve.memset(acc[:, :, :], 0.0)
            dve.memset(top[:, :, :], 0.0)
            dve.memset(WeT[:, :, :], 0.0).then_inc(consts_dve, 1)
            dve.wait_ge(l_in, 3 * 16)
            dve.tensor_tensor(restart_l[:, :], dst_l[:, :], prev_l[:, :], ALU.not_equal).then_inc(ends_found, 1)
            dve.wait_ge(ends_found, 1)
            dve.tensor_scalar(restart_l[:, :], restart_l[:, :], NEG, None, ALU.mult).then_inc(restart_ready, 1)
            dve.wait_ge(ix_in, 7 * 16)
            dve.tensor_tensor(inner[:, :, :], dst_i[:, :, :], next_i[:, :, :], ALU.is_equal).then_inc(ends_ready, 1)
            dve.wait_ge(ends_ready, 1)
            dve.scalar_tensor_tensor(end_i[:, :, :], inner[:, :, :], float(NO_ROW), dst_i[:, :, :],
                                     ALU.mult, ALU.add).then_inc(ends_ready, 1)
            dve.wait_ge(b2_in, 16)
            for k in range(1, 4):
                dve.tensor_copy(b2_rep[:, k * D:(k + 1) * D], b2_rep[:, 0:D]).then_inc(b2_split, 1)
            dve.wait_ge(b2_split, 3)
            dve.tensor_copy(b2_part[:, 0], b2_rep[:, :]).then_inc(b2_split, 1)
            dve.wait_ge(b2_split, 4)
            dve.tensor_tensor(b2_rest[:, 0], b2_rep[:, :], b2_part[:, 0], ALU.subtract).then_inc(b2_split, 1)
            dve.wait_ge(b2_split, 5)
            dve.tensor_copy(b2_part[:, 1], b2_rest[:, 0]).then_inc(b2_split, 1)
            dve.wait_ge(b2_split, 6)
            dve.tensor_tensor(b2_rest[:, 1], b2_rest[:, 0], b2_part[:, 1], ALU.subtract).then_inc(b2_split, 1)
            dve.wait_ge(b2_split, 7)
            dve.tensor_copy(b2_part[:, 2], b2_rest[:, 1]).then_inc(b2_split, 1)
            dve.wait_ge(b2_split, 8)
            dve.wait_ge(consts_dve, 1)
            for k in range(3):
                dve.tensor_copy(b2_rows[32 * k:32 * k + 1, :], b2_part[32 * k:32 * k + 1, k]).then_inc(b2_split, 1)
            dve.wait_ge(setup_ps, 1)
            dve.tensor_scalar(WqT[:, :], E0[:, 0:P], 1.0 / np.sqrt(CH), None, ALU.mult)
            for k, w in enumerate((WkT, WvT, WdT)):
                dve.tensor_copy(w[:, :], E0[:, (k + 1) * P:(k + 2) * P])
            for j in range(ET):
                last = dve.tensor_copy(WeT[KA * j:KA * (j + 1), j], E1[KA * j:KA * (j + 1), 0:P])
            last.then_inc(setup_sb, 1)
            dve.wait_ge(setup_ps, 2)
            dve.tensor_tensor(Wh[:, :], E2[:, 0:P], W1a[:, :], ALU.add)
            dve.wait_ge(col_in, 3 * 16)
            dve.tensor_tensor(cols[:, 3:4], E3[:, 0:1], cols[:, 1:2], ALU.add).then_inc(setup_sb, 1)

            def norm_stats(row, tiles):
                for t in tiles:
                    ins = dve.bn_stats(stats[:, t], row(t))
                return ins

            ROOT0 = 4
            LAST = ROOT0 + 3 * ROOT_STEPS

            def scales(stage, mine, batch, p, a, b, free=()):
                w = slice(a, b)
                dve.wait_ge(mine, batch * LAST + stage + 1)
                if stage == 0:
                    m0, m1, v0, v1 = stats[:, w, 1], stats[:, w, 4], stats[:, w, 2], stats[:, w, 5]
                    dve.tensor_tensor(sums[:, w], m0, m1, ALU.add)
                    dve.tensor_tensor(diff[:, w], m0, m1, ALU.subtract)
                    ins = dve.tensor_tensor(q4[:, w], v0, v1, ALU.add)
                elif stage == 1:
                    dve.scalar_tensor_tensor(sq[:, w], diff[:, w], 0.25, diff[:, w], ALU.mult, ALU.mult)
                    ins = dve.tensor_scalar(q4[:, w], q4[:, w], 1.0 / D, EPS, ALU.mult, ALU.add)
                elif stage == 2:
                    ins = dve.tensor_tensor(var[:, w], q4[:, w], sq[:, w], ALU.add)
                elif stage == 3:
                    dve.tensor_scalar(guess[:, w].bitcast(I32), var[:, w].bitcast(I32), 1, None,
                                      ALU.logical_shift_right).then_inc(half_ok, 1)
                    dve.wait_ge(half_ok, batch + 1 + (STEPS + 1 if mine is lnB else 0))
                    ins = dve.tensor_scalar(root[:, w].bitcast(I32), guess[:, w].bitcast(I32), -1.0,
                                            float(ROOT_BITS), ALU.mult, ALU.add)
                elif (stage - ROOT0) % 3 == 0:
                    ins = dve.tensor_tensor(root_t[:, w], root[:, w], root[:, w], ALU.mult)
                elif (stage - ROOT0) % 3 == 1:
                    ins = dve.scalar_tensor_tensor(root_u[:, w], root_t[:, w], -0.5, var[:, w], ALU.mult, ALU.mult)
                else:
                    y = root[:, w]
                    if stage == LAST - 1:
                        y = rstd[:, p, w]
                        for sem_, n in free:
                            dve.wait_ge(sem_, n)
                    ins = dve.scalar_tensor_tensor(y, root_u[:, w], 1.5, root[:, w], ALU.add, ALU.mult)
                if stage < LAST - 1:
                    ins.then_inc(mine, 1)
                else:
                    ins.then_inc(root_ok, 1)

            def shifts(done, roots, p, a, b):
                w = slice(a, b)
                dve.wait_ge(root_ok, roots)
                dve.scalar_tensor_tensor(shift[:, p, w], sums[:, w], -0.5, rstd[:, p, w],
                                         ALU.mult, ALU.mult).then_inc(done, 1)

            def norm_rows(s, tiles, row):
                for t in tiles:
                    ins = dve.tensor_scalar(h[:, s.par, t], row(t), rstd[:, s.par, t:t + 1], shift[:, s.par, t:t + 1],
                                            ALU.mult, ALU.add)
                return ins

            edge_tiles = range(NT, NL)
            dve_tiles = range(ACT_TILES, NL)

            def edge_stats(s):
                dve.wait_ge(xs_got[s.par], 16 * ET * (s.i + 1))
                dve.wait_ge(xd_got[s.par], 16 * ET * (s.i + 1))
                return norm_stats(lambda t: row_of(s, t), edge_tiles)

            def node_stats(s, halves=range(2)):
                for half in halves:
                    dve.wait_ge(x_loaded[half][s.par], 16 * (s.i + 1))
                    ins = norm_stats(lambda t: row_of(s, t), range(half * NT // 2, (half + 1) * NT // 2))
                return ins

            def edge_rows(s):
                norm_rows(s, dve_tiles, lambda t: row_of(s, t)).then_inc(edges_normed, 1)

            def products(s):
                dve.wait_ge(k_ps, s.c + 1)
                dve.wait_ge(q_ok, s.c + 1)
                dve.wait_ge(s_ps, s.c)
                dve.tensor_tensor(qk[:, :], q_sb[:, :], E2[:, :], ALU.mult).then_inc(qk_ok, 1)

            edge_stats(step(0)).then_inc(ln, 1)
            for k in range(LAST):
                scales(k, ln, 0, 0, NT, NL)
            shifts(scales_ready, 1, 0, NT, NL)
            dve.wait_ge(scales_ready, 1)
            edge_rows(step(0))
            node_stats(step(0))
            edge_stats(step(1)).then_inc(ln, 1)
            for k in range(LAST):
                scales(k, ln, 1, 1, 0, NL)
            shifts(scales_ready, 2, 1, 0, NL)
            dve.wait_ge(scales_ready, 2)
            edge_rows(step(1))
            products(step(0))

            def add_rows(s, k):
                if k == 0:
                    dve.wait_ge(out_stored[s.par], 16 * s.i)
                dve.wait_ge(o_ps, DT * s.c + k + 1)
                dve.tensor_tensor(x_out[:, s.par, ET * k:ET * (k + 1)],
                                  O_ps[:, :].rearrange("p (j d) -> p j d", j=ET),
                                  x_in[:, s.par, ET * k:ET * (k + 1)], ALU.add).then_inc(out_ok, 1)

            SEAM = FULL * EC - (E - EC)

            def phase_a(s):
                nxt, far = step(s, 1), step(s, 2)
                before = EC - 1 - SEAM if s.last else EC - 1
                seam = EC - 1 - SEAM if isinstance(s.i, int) and s.c == FULL - 1 else EC - 1
                tiles = (0 if nxt else NT, NL if far else NT)

                def scale(*stages):
                    for k in stages:
                        if nxt:
                            scales(k, ln, s.c + 2, s.par, *tiles, free=[(nodes_normed, DT * s.c), (edges_normed_act, s.c + 1)])

                if far:
                    edge_stats(far)
                dve.wait_ge(s_ok, s.c + 1)
                dve.wait_ge(restart_loaded[s.par], 16 * (s.i + 1))
                dve.wait_ge(carried, s.c)
                dve.wait_ge(rden_ok, s.c)
                dve.tensor_tensor_scan(E3[:, :], restart[:, s.par], s_sb[:, :], carry[:, 0:1],
                                       ALU.add, ALU.max).then_inc(max_ok, 1)
                dve.wait_ge(max_ok, s.c + 1)
                dve.tensor_tensor(ga[:, 0:1], restart[:, s.par, 0:1], carry[:, 0:1], ALU.add)
                dve.tensor_tensor(ga[:, 1:EC], restart[:, s.par, 1:EC], E3[:, 0:EC - 1], ALU.add).then_inc(gap0_ok, 1)
                dve.tensor_tensor(gb[:, :], s_sb[:, :], E3[:, :], ALU.subtract)
                dve.wait_ge(gap0_ok, s.c + 1)
                dve.tensor_copy(carry[:, 0:1], E3[:, seam:seam + 1]).then_inc(carried, 1)
                dve.tensor_tensor(ga[:, :], ga[:, :], E3[:, :], ALU.subtract).then_inc(gaps_ok, 1)
                if nxt:
                    node_stats(nxt).then_inc(ln, 1)
                    products(nxt)
                scale(0)
                add_rows(s, 0)
                scale(1)
                dve.wait_ge(exp_ok, s.c + 1)
                dve.tensor_tensor_scan(den[:, s.par], ga[:, :], gb[:, :], den[:, 1 - s.par, before:before + 1],
                                       ALU.mult, ALU.add).then_inc(den_ok, 1)
                scale(2)
                dve.wait_ge(v_ps, s.c + 1)
                dve.tensor_tensor(bv[:, :], gb[:, :], E4[:, :], ALU.mult).then_inc(bv_ok, 1)
                scale(3)
                dve.wait_ge(bv_ok, s.c + 1)
                dve.tensor_tensor_scan(acc[:, s.par], ga[:, :], bv[:, :], acc[:, 1 - s.par, before:before + 1],
                                       ALU.mult, ALU.add).then_inc(acc_ok, 1)
                scale(4)
                add_rows(s, 1)
                scale(5, 6, 7)
                dve.wait_ge(den_ps, s.c + 1)
                dve.reciprocal(rden[:, :, :], E3[:, :].rearrange("p (j g r) -> p j g r", j=ET, r=CH)[:, :, :, 0]
                               ).then_inc(rden_ok, 1)
                scale(8)
                dve.wait_ge(rden_ok, s.c + 1)
                dve.wait_ge(acc_ps, s.c + 1)
                heads = E4[:, :].rearrange("p (g r) -> p g r", r=CH)
                dve.tensor_tensor(heads, heads, rden[:, :, :].rearrange("p j g -> p (j g)").unsqueeze(2)
                                  .broadcast_to([P, ET * HEADS, CH]), ALU.mult).then_inc(att_ok, 1)
                scale(9, 10)
                dve.wait_ge(att_ok, s.c + 1)
                dve.wait_ge(xd_copied, s.c + 1)
                dve.wait_ge(x1_stored[s.par], 16 * s.i)
                dve.tensor_tensor(x1[:, s.par], E4[:, :].rearrange("p (j d) -> p j d", j=ET),
                                  xd_kept[:, s.par], ALU.add).then_inc(x1_ok, 1)
                scale(*range(11, LAST))
                if nxt:
                    shifts(scales_ready, s.c + 3, s.par, *tiles)
                add_rows(s, 2)
                if far:
                    dve.wait_ge(scales_ready, s.c + 3)
                    dve.wait_ge(hdT_ps, s.c + 1)
                    edge_rows(far)
                add_rows(s, 3)

            run(dve, phase_a)

            def stats_b(s):
                dve.wait_ge(ys_replaced[s.par], 16 * ET * (s.i + 1))
                dve.wait_ge(yd_loaded[s.par], 16 * (s.i + 1))
                norm_stats(lambda t: row_of(s, t), edge_tiles).then_inc(lnB, 1)

            A_BATCHES = STEPS + 1
            for c in range(2):
                stats_b(step(c))
                for k in range(LAST):
                    scales(k, lnB, c, c, NT, NL)
                shifts(scalesB, A_BATCHES + c + 1, c, NT, NL)

            def phase_b(s):
                far = step(s, 2)
                before = EC - 1 - SEAM if s.last else EC - 1

                def scale(*stages):
                    for k in stages:
                        if far:
                            scales(k, lnB, s.c + 2, s.par, NT, NL, [(normedB, s.c + 1)])

                dve.wait_ge(m_ps, s.c + 1)
                dve.wait_ge(ew_loaded[s.par], 16 * (s.i + 1))
                dve.scalar_tensor_tensor(msg[:, :], ew[:, s.par], cols[:, 2:3], E2[:, :],
                                         ALU.mult, ALU.add).then_inc(msg_ok, 1)
                dve.wait_ge(msg_ok, s.c + 1)
                dve.wait_ge(restartB_loaded[s.par], 16 * (s.i + 1))
                dve.wait_ge(g_ps, s.c)
                dve.tensor_tensor_scan(top[:, s.par], restart[:, s.par], msg[:, :], top[:, 1 - s.par, before:before + 1],
                                       ALU.add, ALU.max).then_inc(top_ok, 1)
                if far:
                    stats_b(far)
                scale(*range(LAST))
                if far:
                    shifts(scalesB, A_BATCHES + s.c + 3, s.par, NT, NL)
                dve.wait_ge(r_ps, s.c + 1)
                dve.wait_ge(out_put[s.par], 16 * ET * s.i)
                dve.wait_ge(ydB_kept, s.c + 1)
                dve.tensor_tensor(x1[:, s.par], E4[:, :].rearrange("p (j d) -> p j d", j=ET),
                                  xd_kept[:, s.par], ALU.add).then_inc(row_ok, 1)

            run(dve, phase_b, LOOPS_B)

        @block.scalar
        def _(act):
            def turned(dst_tile, src_bank, func=ACT.Relu):
                return act.activation(dst_tile.rearrange("f (p j) -> f j p", j=ET),
                                      src_bank[:, :].rearrange("f (j p) -> f j p", j=ET), func)

            def normalise(s, tiles, p):
                for t in tiles:
                    row = (x_in[:, s.par, t] if t < NT else xs[:, s.par, t - NT] if t < NT + ET
                           else xd[:, s.par, t - NT - ET])
                    ins = act.activation(h[:, s.par, t], row, ACT.Relu, bias=shift[:, p, t:t + 1],
                                         scale=rstd[:, p, t:t + 1])
                return ins

            def keep_xd(s):
                act.wait_ge(xd_got[s.par], 16 * ET * (s.i + 1))
                act.activation(xd_kept[:, s.par], xd[:, s.par], ACT.Copy).then_inc(xd_copied, 1)

            act_edges = range(NT, ACT_TILES)

            def edge_columns(s):
                act.wait_ge(hsT_ps, s.c + 1)
                if not (isinstance(s.i, int) and s.c == 0):
                    act.wait_ge(v_ps, s.c - 1)
                turned(hsT[:, s.par], E0).then_inc(hsT_ok, 1)
                act.wait_ge(hdT_ps, s.c + 1)
                act.wait_ge(q_ps, s.c)
                turned(hdT[:, 0], E1).then_inc(hdT_ok, 1)
                act.wait_ge(attrT_ps, s.c + 1)
                act.wait_ge(s_ps, s.c)
                act.activation(attrT[:, :], E2[:, 0:P], ACT.Copy).then_inc(attrT_ok, 1)

            def queries(s):
                act.wait_ge(q_ps, s.c + 1)
                act.wait_ge(qk_ok, s.c)
                act.activation(q_sb[:, :], E1[:, :], ACT.Copy).then_inc(q_ok, 1)

            def scores(s):
                act.wait_ge(s_ps, s.c + 1)
                act.wait_ge(gaps_ok, s.c)
                act.activation(s_sb[:, :], E0[:, :], ACT.Copy).then_inc(s_ok, 1)

            def part(s, k):
                normalise(s, range(ET * k, ET * (k + 1)), 1 - s.par).then_inc(nodes_normed, 1)

            act.wait_ge(scales_ready, 1)
            normalise(step(0), act_edges, 0).then_inc(edges_normed_act, 1)
            keep_xd(step(0))
            edge_columns(step(0))
            queries(step(0))
            act.wait_ge(scales_ready, 2)
            part(step(0), 0)
            normalise(step(1), act_edges, 1).then_inc(edges_normed_act, 1)
            scores(step(0))
            keep_xd(step(1))

            def phase_a(s):
                nxt, far = step(s, 1), step(s, 2)

                def evac_h(k):
                    n = DT * s.c + k
                    act.wait_ge(hT_ps, n + 1)
                    act.wait_ge(hid_ps, n - 1 if k else n)
                    act.activation(hT[:, k % 2], T_ps[:, :], ACT.Relu).then_inc(hT_ok, 1)

                def evac_hid(k):
                    n = DT * s.c + k
                    act.wait_ge(hid_ps, n + 1)
                    act.wait_ge(o_ps, n - 1 if k else n)
                    act.activation(hid[:, k % 2], H_ps[:, :], ACT.Relu, bias=cols[:, 1:2]).then_inc(hid_ok, 1)

                evac_h(0)
                if nxt:
                    edge_columns(nxt)
                part(s, 1)
                act.wait_ge(gaps_ok, s.c + 1)
                act.activation(ga[:, :], ga[:, :], ACT.Exp)
                act.activation(gb[:, :], gb[:, :], ACT.Exp).then_inc(exp_ok, 1)
                evac_hid(0)
                evac_h(1)
                if nxt:
                    queries(nxt)
                part(s, 2)
                evac_hid(1)
                evac_h(2)
                if nxt:
                    scores(nxt)
                part(s, 3)
                evac_hid(2)
                evac_h(3)
                evac_hid(3)
                if nxt:
                    act.wait_ge(scales_ready, s.c + 3)
                    act.wait_ge(hT_ps, DT * s.c)
                    part(nxt, 0)
                if far:
                    act.wait_ge(hdT_ps, s.c + 1)
                    normalise(far, act_edges, s.par).then_inc(edges_normed_act, 1)
                    act.wait_ge(x1_ok, s.c + 1)
                    keep_xd(far)

            run(act, phase_a)

            def columns_b(s):
                act.wait_ge(ysT_ps, s.c + 1)
                act.wait_ge(m_ps, s.c)
                turned(hsT[:, 0], E0).then_inc(ysT_ok, 1)
                act.wait_ge(ydT_ps, s.c + 1)
                if not (isinstance(s.i, int) and s.c == 0):
                    act.wait_ge(g_ps, s.c - 1)
                turned(hdT[:, s.par], E1).then_inc(ydT_ok, 1)

            def keep_yd(s):
                act.wait_ge(yd_loaded[s.par], 16 * (s.i + 1))
                act.activation(xd_kept[:, s.par], xd[:, s.par], ACT.Copy).then_inc(ydB_kept, 1)

            keep_yd(step(0))
            for c in range(2):
                act.wait_ge(scalesB, c + 1)
                normalise(step(c), range(NT, NL), c).then_inc(normedB, 1)
            columns_b(step(0))

            def phase_b(s):
                nxt, far = step(s, 1), step(s, 2)
                if nxt:
                    columns_b(nxt)
                    act.wait_ge(row_ok, s.c)
                    keep_yd(nxt)
                act.wait_ge(g_ps, s.c + 1)
                act.wait_ge(r_ps, s.c)
                act.activation(hidB[:, :], E3[:, :], ACT.Relu, bias=cols[:, 3:4]).then_inc(g_ok, 1)
                if far:
                    act.wait_ge(scalesB, s.c + 3)
                    act.wait_ge(ydT_ps, s.c + 1)
                    normalise(far, range(NT, NL), s.par).then_inc(normedB, 1)

            run(act, phase_b, LOOPS_B)

        @block.tensor
        def _(pe):
            pe.wait_ge(consts_pool, 6)
            pe.wait_ge(w_in, 16 * 16)
            for n in range(4):
                pe.transpose(E0[:, n * P:(n + 1) * P], wload[:, n], ident[:, :])
            pe.transpose(E1[:, 0:P], we_rows[:, :, :].rearrange("p j k -> p (j k)"), ident[:, :]).then_inc(setup_ps, 1)
            pe.wait_ge(setup_sb, 1)
            pe.wait_ge(col_in, 3 * 16)
            pe.matmul(E2[:, 0:P], WdT[:, :], W1b[:, :], start=True, stop=True)
            pe.matmul(E3[:, 0:1], W1b[:, :], cols[:, 0:1], start=True, stop=True).then_inc(setup_ps, 1)
            pe.wait_ge(setup_sb, 2)
            pe.wait_ge(b2_split, 11)

            def turn(bank_, s, first):
                for j in range(ET):
                    ins = pe.transpose(bank_[:, j * P:(j + 1) * P], h[:, s.par, first + j], ident[:, :])
                return ins

            def rows_out(bank_, hidden):
                pe.matmul(bank_[:, :], ones_bf[:, :], b2_rows[:, :], start=True, stop=False, skip_group_check=True)
                for j in range(ET):
                    ins = pe.matmul(bank_[:, j * P:(j + 1) * P], hidden(j), W2s[:, :],
                                    start=False, stop=True, skip_group_check=True)
                return ins

            def edge_columns(s):
                pe.wait_ge(edges_normed, s.c + 1)
                pe.wait_ge(edges_normed_act, s.c + 1)
                pe.wait_ge(s_ok, s.c)
                turn(E0, s, NT).then_inc(hsT_ps, 1)
                pe.wait_ge(q_ok, s.c)
                turn(E1, s, NT + ET).then_inc(hdT_ps, 1)
                pe.wait_ge(attr_loaded[s.par], 16 * (s.i + 1))
                pe.wait_ge(qk_ok, s.c)
                pe.transpose(E2[:, 0:P], attr[:, s.par].rearrange("p j k -> p (j k)"), ident[:, :]).then_inc(attrT_ps, 1)

            def queries_keys(s):
                pe.wait_ge(hdT_ok, s.c + 1)
                pe.matmul(E1[:, :], WqT[:, :], hdT[:, 0], start=True, stop=True).then_inc(q_ps, 1)
                pe.wait_ge(hsT_ok, s.c + 1)
                pe.wait_ge(attrT_ok, s.c + 1)
                pe.matmul(E2[:, :], WkT[:, :], hsT[:, s.par], start=True, stop=True).then_inc(k_ps, 1)

            def scores(s):
                pe.wait_ge(qk_ok, s.c + 1)
                pe.matmul(E0[:, :], head_sum[:, :], qk[:, :], start=True, stop=False, skip_group_check=True)
                for j in range(ET):
                    ins = pe.matmul(E0[:, j::ET], WeT[:, j], attrT[:, :], start=False, stop=True, skip_group_check=True)
                ins.then_inc(s_ps, 1)

            edge_columns(step(0))
            queries_keys(step(0))
            scores(step(0))

            def phase_a(s):
                nxt = step(s, 1)

                def turn_h(k):
                    pe.wait_ge(nodes_normed, DT * s.c + k + 1)
                    pe.wait_ge(hT_ok, DT * s.c + k)
                    turn(T_ps, s, ET * k).then_inc(hT_ps, 1)

                def hidden(k):
                    n = DT * s.c + k
                    pe.wait_ge(hT_ok, n + 1)
                    pe.wait_ge(hid_ok, n)
                    pe.matmul(H_ps[:, :], W1a[:, :], hT[:, k % 2], start=True, stop=True).then_inc(hid_ps, 1)

                def second(k):
                    n = DT * s.c + k
                    pe.wait_ge(hid_ok, n + 1)
                    pe.wait_ge(out_ok, n)
                    rows_out(O_ps, lambda j: hid[:, k % 2, j * P:(j + 1) * P]).then_inc(o_ps, 1)

                pe.wait_ge(x1_ok, s.c)
                pe.wait_ge(hsT_ok, s.c + 1)
                pe.matmul(E4[:, :], WvT[:, :], hsT[:, s.par], start=True, stop=True).then_inc(v_ps, 1)
                turn_h(0)
                if nxt:
                    edge_columns(nxt)
                hidden(0)
                turn_h(1)
                if nxt:
                    queries_keys(nxt)
                hidden(1)
                second(0)
                turn_h(2)
                if nxt:
                    scores(nxt)
                hidden(2)
                second(1)
                pe.wait_ge(acc_ok, s.c + 1)
                for j in range(ET):
                    ins = pe.transpose(E3[:, j * P:(j + 1) * P], den[:, s.par, j::ET], ident[:, :])
                ins.then_inc(den_ps, 1)
                for j in range(ET):
                    ins = pe.transpose(E4[:, j * P:(j + 1) * P], acc[:, s.par, j::ET], ident[:, :])
                ins.then_inc(acc_ps, 1)
                turn_h(3)
                hidden(3)
                second(2)
                second(3)

            run(pe, phase_a)

            pe.wait_ge(x1_ok, STEPS)

            def columns_b(s):
                pe.wait_ge(normedB, s.c + 1)
                pe.wait_ge(ysT_ok, s.c)
                turn(E0, s, NT).then_inc(ysT_ps, 1)
                pe.wait_ge(ydT_ok, s.c)
                turn(E1, s, NT + ET).then_inc(ydT_ps, 1)

            def messages(s):
                pe.wait_ge(ysT_ok, s.c + 1)
                pe.wait_ge(msg_ok, s.c)
                pe.matmul(E2[:, :], Ws[:, :], hsT[:, 0], start=True, stop=True).then_inc(m_ps, 1)

            columns_b(step(0))
            messages(step(0))

            def phase_b(s):
                nxt = step(s, 1)
                if nxt:
                    columns_b(nxt)
                pe.wait_ge(ydT_ok, s.c + 1)
                pe.wait_ge(g_ok, s.c)
                pe.matmul(E3[:, :], Wh[:, :], hdT[:, s.par], start=True, stop=False)
                if nxt:
                    messages(nxt)
                pe.wait_ge(top_ok, s.c + 1)
                pe.matmul(E3[:, :], W1b[:, :], top[:, s.par], start=False, stop=True).then_inc(g_ps, 1)
                pe.wait_ge(g_ok, s.c + 1)
                pe.wait_ge(row_ok, s.c)
                rows_out(E4, lambda j: hidB[:, j::ET]).then_inc(r_ps, 1)

            run(pe, phase_b, LOOPS_B)


_INS = ["x", "src", "dst", "edge_attr_32", "edge_weight", "L0_gnn_Wq", "L0_gnn_Wk", "L0_gnn_Wv", "L0_gnn_We",
        "L1_gnn_Wm", "L1_gnn_bm", "L1_gnn_W1", "L1_gnn_b1", "L1_gnn_W2", "L1_gnn_b2"]


def kernel(**inputs):
    import concourse.bacc as bacc
    from concourse.bass_utils import run_bass_kernel_spmd

    nc = bacc.Bacc("TRN2", target_bir_lowering=False, num_devices=1)
    arrays, args = {}, []
    for name in _INS:
        a = np.ascontiguousarray(inputs[name])
        arrays[f"in_{name}"] = a
        args.append(nc.dram_tensor(f"in_{name}", a.shape, mybir.dt.from_np(a.dtype), kind="ExternalInput").ap())
    shape = inputs["x"].shape
    args.append(nc.dram_tensor("out_x", shape, F32, kind="ExternalOutput").ap())
    gnn_two_layers(nc, *args)
    return run_bass_kernel_spmd(nc, [arrays], core_ids=[0]).results[0]["out_x"]
```

```python
from contextlib import ExitStack

import numpy as np

import concourse.bass as bass
from concourse import mybir

F32 = mybir.dt.float32
BF16 = mybir.dt.bfloat16
I32 = mybir.dt.int32
U32 = mybir.dt.uint32
ALU = mybir.AluOpType
ACT = mybir.ActivationFunctionType

P = 128
D = 128
HEADS = 8
CH = D // HEADS
KA = 32
ET = 4
EC = ET * P
NT = 16
NCH = NT * P
DT = NT // ET
NL = NT + 2 * ET
ACT_TILES = 20
ROOT_STEPS = 3
ROOT_BITS = 0x5F3759DF
EPS = 1e-5
NEG = -3.0e38
NO_ROW = 1 << 20


class Step:

    def __init__(self, i, par, last, n_edges, n_nodes):
        self.i, self.par, self.last = i, par, last
        self.c = i * 2 + par
        self.edge0 = n_edges - EC if last else i * (2 * EC) + par * EC
        self.node0 = n_nodes - NCH if last else i * (2 * NCH) + par * NCH

    def edges(self):
        return bass.ds(self.edge0, EC)

    def nodes(self):
        return bass.ds(self.node0, NCH)


def gnn_two_layers(nc, x, src, dst, edge_attr, edge_weight, Wq, Wk, Wv, We, Wm, bm, W1, b1, W2, b2, out):
    N, E = x.shape[0], src.shape[0]
    STEPS = -(-E // EC)
    assert STEPS == -(-N // NCH) and STEPS % 2 == 1
    FULL = STEPS - 1
    LOOPS = (FULL - 2) // 2
    LOOPS_B = LOOPS - 1
    TABLE_KEPT = FULL // 2
    EPP = E // 125

    def step(c, k=0):
        if isinstance(c, Step):
            if isinstance(c.i, int):
                return step(c.c + k)
            p = c.par + k
            return Step(c.i + p // 2, p % 2, False, E, N)
        n = c + k
        return Step(n // 2, n % 2, n == FULL, E, N) if n <= FULL else None

    def run(eng, body, rounds=LOOPS):
        for c in range(2):
            body(step(c))
        with eng.Fori(1, rounds) as i:
            for par in range(2):
                body(Step(i, par, False, E, N))
        for c in range(2 * rounds, STEPS):
            body(step(c))

    with ExitStack() as ctx:
        def sb(name, shape, dt=F32):
            return ctx.enter_context(nc.sbuf_tensor(name, shape, dt))

        def sem(name):
            return ctx.enter_context(nc.semaphore(name))

        def sem2(name):
            return [sem(f"{name}_{p}") for p in range(2)]

        bank = [ctx.enter_context(nc.psum_tensor(f"bank{b}", [P, 512], F32)) for b in range(8)]
        T_ps, H_ps, O_ps, E0, E1, E2, E3, E4 = bank

        restart_row = nc.dram_tensor("restart_row", [E], F32).ap()
        last_edge = nc.dram_tensor("last_edge", [N, 1], I32).ap()
        xs_rows = nc.dram_tensor("xs_rows", [E, D], F32).ap()
        x1_rows = nc.dram_tensor("x1_rows", [E, D], F32).ap()

        ident = sb("ident", [P, P])
        head_sum = sb("head_sum", [P, P])
        wload = sb("wload", [P, 4, P])
        we_rows = sb("we_rows", [P, ET, KA])
        WqT, WkT, WvT, WdT = (sb(n, [P, P]) for n in ("WqT", "WkT", "WvT", "WdT"))
        WeT = sb("WeT", [P, ET, P])
        Ws = sb("Ws", [P, P])
        W1a, W1b, W2s, Wh = (sb(n, [P, P]) for n in ("W1a", "W1b", "W2s", "Wh"))
        cols = sb("cols", [P, 4])
        b2_rep = sb("b2_rep", [P, 512])
        b2_part = sb("b2_part", [P, 3, 512], BF16)
        b2_rest = sb("b2_rest", [P, 2, 512])
        b2_rows = sb("b2_rows", [P, 512], BF16)
        ones_bf = sb("ones_bf", [P, P], BF16)

        edge_ix = sb("edge_ix", [P, STEPS, 2, ET], I32)
        src_i, dst_i = edge_ix[:, :, 0, :], edge_ix[:, :, 1, :]
        next_i = sb("next_i", [P, STEPS, ET], I32)
        inner = sb("inner", [P, STEPS, ET])
        end_i = sb("end_i", [P, STEPS, ET], I32)
        edge_i = sb("edge_i", [P, STEPS, ET], I32)
        found = sb("found", [P, STEPS, ET], I32)
        dst_l = sb("dst_l", [125, EPP], I32)
        prev_l = sb("prev_l", [125, EPP], I32)
        restart_l = sb("restart_l", [125, EPP])
        no_rows = sb("no_rows", [125, N // 125], I32)
        gather_ix = sb("gather_ix", [P, 2, 2, ET], I32)
        table_ix = sb("table_ix", [P, 2, 2, 2 * ET], I32)
        table_got = sb("table_got", [P, 2, 2 * ET], I32)

        x_in = sb("x_in", [P, 2, NT, D])
        x_out = sb("x_out", [P, 2, NT, D])
        h = sb("h", [P, 2, NL, D])
        xs = sb("xs", [P, 2, ET, D])
        xd = sb("xd", [P, 2, ET, D])
        xd_kept = sb("xd_kept", [P, 2, ET, D])
        x1 = sb("x1", [P, 2, ET, D])
        attr = sb("attr", [P, 2, ET, KA])
        restart = sb("restart", [P, 2, EC])
        ew = sb("ew", [P, 2, EC])
        stats = sb("stats", [P, NL, 6])
        sums, diff, q4, sq, var, guess, root, root_t, root_u = (sb(n, [P, NL]) for n in (
            "sums", "diff", "q4", "sq", "var", "guess", "root", "root_t", "root_u"))
        rstd, shift = sb("rstd", [P, 2, NL]), sb("shift", [P, 2, NL])
        hsT, hdT = sb("hsT", [P, 2, EC]), sb("hdT", [P, 2, EC])
        q_sb, qk, s_sb = (sb(n, [P, EC]) for n in ("q_sb", "qk", "s_sb"))
        attrT = sb("attrT", [P, P])
        ga, gb, bv = (sb(n, [P, EC]) for n in ("ga", "gb", "bv"))
        den, acc = sb("den", [P, 2, EC]), sb("acc", [P, 2, EC])
        rden = sb("rden", [P, ET, HEADS])
        carry = sb("carry", [P, 1])
        hT = sb("hT", [P, 2, 512])
        hid = sb("hid", [P, 2, 512])
        msg = sb("msg", [P, EC])
        top = sb("top", [P, 2, EC])
        hidB = sb("hidB", [P, EC])

        w_in, col_in, b2_in, ix_in, next_in, l_in = (sem(n) for n in
                                                    ("w_in", "col_in", "b2_in", "ix_in", "next_in", "l_in"))
        consts_pool, consts_dve = sem("consts_pool"), sem("consts_dve")
        setup_ps, setup_sb = sem("setup_ps"), sem("setup_sb")
        b2_split = sem("b2_split")
        restart_ready, restart_stored = sem("restart_ready"), sem("restart_stored")
        ends_ready, table_cleared = sem("ends_ready"), sem("table_cleared")
        no_rows_ready, ends_found = sem("no_rows_ready"), sem("ends_found")
        x_loaded = [sem2(f"x_loaded_{half}") for half in range(2)]
        attr_loaded, restart_loaded = sem2("attr_loaded"), sem2("restart_loaded")
        xs_got, xd_got = sem2("xs_got"), sem2("xd_got")
        xs_stored, x1_stored, out_stored = sem2("xs_stored"), sem2("x1_stored"), sem2("out_stored")
        table_put, table_read = sem2("table_put"), sem2("table_read")
        ys_loaded, yd_loaded, ew_loaded, restartB_loaded = (sem2(n) for n in
                                                            ("ys_loaded", "yd_loaded", "ew_loaded", "restartB_loaded"))
        ys_replaced, out_put = sem2("ys_replaced"), sem2("out_put")
        gate, sp_gate = sem("gate"), sem("sp_gate")
        ix_staged, table_staged, found_kept = sem("ix_staged"), sem("table_staged"), sem("found_kept")
        ln = sem("ln")
        half_ok, root_ok = sem("half_ok"), sem("root_ok")
        scales_ready = sem("scales_ready")
        nodes_normed, edges_normed, edges_normed_act = sem("nodes_normed"), sem("edges_normed"), sem("edges_normed_act")
        xd_copied = sem("xd_copied")
        hsT_ps, hdT_ps, attrT_ps, q_ps, k_ps, v_ps, s_ps, acc_ps, den_ps = (sem(n) for n in
            ("hsT_ps", "hdT_ps", "attrT_ps", "q_ps", "k_ps", "v_ps", "s_ps", "acc_ps", "den_ps"))
        hsT_ok, hdT_ok, attrT_ok, q_ok, s_ok = (sem(n) for n in ("hsT_ok", "hdT_ok", "attrT_ok", "q_ok", "s_ok"))
        hT_ps, hid_ps, o_ps, hT_ok, hid_ok, out_ok = (sem(n) for n in
            ("hT_ps", "hid_ps", "o_ps", "hT_ok", "hid_ok", "out_ok"))
        qk_ok, max_ok, gap0_ok, gaps_ok, carried = (sem(n) for n in ("qk_ok", "max_ok", "gap0_ok", "gaps_ok", "carried"))
        exp_ok, den_ok, bv_ok, acc_ok, rden_ok, att_ok, x1_ok = (sem(n) for n in
            ("exp_ok", "den_ok", "bv_ok", "acc_ok", "rden_ok", "att_ok", "x1_ok"))
        x1_all_stored, out_all_stored = sem("x1_all_stored"), sem("out_all_stored")
        lnB, scalesB, ysB_normed, ydB_normed, ydB_kept = (sem(n) for n in
            ("lnB", "scalesB", "ysB_normed", "ydB_normed", "ydB_kept"))
        ysT_ps, ydT_ps, m_ps, g_ps, r_ps = (sem(n) for n in ("ysT_ps", "ydT_ps", "m_ps", "g_ps", "r_ps"))
        ysT_ok, ydT_ok, msg_ok, top_ok, g_ok, row_ok = (sem(n) for n in
            ("ysT_ok", "ydT_ok", "msg_ok", "top_ok", "g_ok", "row_ok"))
        ixB_staged = sem("ixB_staged")

        attr_v = lambda s: edge_attr[s.edges(), :].rearrange("(p j) k -> p j k", j=ET)
        rows_v = lambda t, s: t[s.edges(), :].rearrange("(p j) d -> p j d", j=ET)
        nodes_v = lambda t, s: t[s.nodes(), :].rearrange("(p j) d -> p j d", j=NT)
        spread = lambda t, s: t[s.edges()].partition_broadcast(P)

        block = ctx.enter_context(nc.Block())

        @block.sync
        def _(sp):
            def load_node_rows(s, half):
                t = slice(half * NT // 2, (half + 1) * NT // 2)
                sp.dma_start(x_in[:, s.par, t], nodes_v(x, s)[:, t]).then_inc(x_loaded[half][s.par], 16)

            def load_attr(s):
                sp.dma_start(attr[:, s.par], attr_v(s)).then_inc(attr_loaded[s.par], 16)

            def load_restart(s, done):
                sp.dma_start(restart[:, s.par], spread(restart_row, s)).then_inc(done[s.par], 16)

            full = FULL * EC
            for tile_, a in ((src_i, src), (dst_i, dst)):
                sp.dma_start(tile_[:, 0:FULL, :], a[0:full].rearrange("(c p j) -> p c j", p=P, j=ET)).then_inc(ix_in, 16)
                sp.dma_start(tile_[:, FULL, :], a[E - EC:E].rearrange("(p j) -> p j", j=ET)).then_inc(ix_in, 16)
            sp.dma_start(dst_l[:, :], dst.rearrange("(p j) -> p j", p=125)).then_inc(l_in, 16)
            sp.wait_ge(consts_pool, 1)
            sp.dma_start(prev_l[0:1, 1:EPP], dst[0:EPP - 1].rearrange("(a j) -> a j", a=1)).then_inc(l_in, 16)
            sp.dma_start(prev_l[1:125, :], dst[EPP - 1:E - 1].rearrange("(p j) -> p j", j=EPP)).then_inc(l_in, 16)
            sp.dma_start(next_i[:, 0:FULL, :], dst[1:full + 1].rearrange("(c p j) -> p c j", p=P, j=ET)).then_inc(next_in, 16)
            sp.dma_start(next_i[0:P - 1, FULL, :], dst[E - EC + 1:E - ET + 1].rearrange("(p j) -> p j", j=ET)).then_inc(next_in, 16)
            sp.dma_start(next_i[P - 1:P, FULL, 0:ET - 1], dst[E - ET + 1:E].rearrange("(a j) -> a j", a=1)).then_inc(next_in, 16)
            sp.dma_start(b2_rep[:, 0:D], b2.partition_broadcast(P)).then_inc(b2_in, 16)
            for half in range(2):
                load_node_rows(step(0), half)
            for n, w in enumerate((Wq, Wk, Wv, Wm[0:D, :])):
                sp.dma_start(wload[:, n], w[:, :]).then_inc(w_in, 16)
            for hd in range(HEADS):
                sp.dma_start(we_rows[CH * hd:CH * (hd + 1)],
                             We[hd:hd + 1, :].unsqueeze(0).broadcast_to([CH, ET, KA])).then_inc(w_in, 16)
            sp.dma_start(Ws[:, :], Wm[D:2 * D, :]).then_inc(w_in, 16)
            sp.dma_start(W1a[:, :], W1[0:D, :]).then_inc(w_in, 16)
            sp.dma_start(W1b[:, :], W1[D:2 * D, :]).then_inc(w_in, 16)
            sp.dma_start(W2s[:, :], W2[:, :]).then_inc(w_in, 16)
            for n, v in enumerate((bm, b1, Wm[2 * D])):
                sp.dma_start(cols[:, n:n + 1], v.rearrange("(p a) -> p a", a=1)).then_inc(col_in, 16)
            load_attr(step(0))
            for half in range(2):
                load_node_rows(step(1), half)
            load_attr(step(1))
            sp.wait_ge(restart_ready, 1)
            sp.dma_start(restart_row.rearrange("(p j) -> p j", p=125), restart_l[:, :]).then_inc(restart_stored, 16)
            sp.wait_ge(no_rows_ready, 1)
            sp.dma_start(last_edge.rearrange("(p j) a -> p (j a)", p=125), no_rows[:, :]).then_inc(table_cleared, 16)
            sp.wait_ge(restart_stored, 16)
            for c in range(2):
                load_restart(step(c), restart_loaded)

            def open_gate():
                sp.sem_inc(sp_gate, 1)

            def store_xs(s):
                if s.last:
                    sp.wait_ge(xs_stored[1 - s.par], 16 * s.i)
                sp.wait_ge(xs_got[s.par], 16 * ET * (s.i + 1))
                open_gate()
                sp.dma_start(rows_v(xs_rows, s), xs[:, s.par]).then_inc(xs_stored[s.par], 16)

            store_xs(step(0))
            store_xs(step(1))

            def phase_a(s):
                far = step(s, 2)
                if far:
                    store_xs(far)
                    sp.wait_ge(attrT_ps, s.c + 1)
                    open_gate()
                    load_attr(far)
                    sp.wait_ge(gaps_ok, s.c + 1)
                    open_gate()
                    load_restart(far, restart_loaded)
                if far:
                    sp.wait_ge(out_ok, DT * s.c + 2)
                    open_gate()
                    load_node_rows(far, 0)
                if s.last:
                    first_loads()
                    store_x1(s)
                    sp.wait_ge(x1_stored[s.par], 16 * (s.i + 1))
                    sp.wait_ge(x1_stored[1 - s.par], 16 * s.i)
                    sp.sem_inc(x1_all_stored, 1)
                    sp.wait_ge(out_stored[1 - s.par], 16 * s.i)
                sp.wait_ge(out_ok, DT * (s.c + 1))
                open_gate()
                if far:
                    load_node_rows(far, 1)
                sp.dma_start(nodes_v(out, s), x_out[:, s.par]).then_inc(out_stored[s.par], 16)
                if not s.last:
                    store_x1(s)

            def store_x1(s):
                if s.last:
                    sp.wait_ge(x1_stored[1 - s.par], 16 * s.i)
                sp.wait_ge(x1_ok, s.c + 1)
                open_gate()
                sp.dma_start(rows_v(x1_rows, s), x1[:, s.par]).then_inc(x1_stored[s.par], 16)

            def load_ys(s):
                sp.dma_start(xs[:, s.par], rows_v(xs_rows, s)).then_inc(ys_loaded[s.par], 16)

            def load_yd(s):
                sp.dma_start(xd[:, s.par], rows_v(x1_rows, s)).then_inc(yd_loaded[s.par], 16)

            def load_ew(s):
                sp.dma_start(ew[:, s.par], spread(edge_weight, s)).then_inc(ew_loaded[s.par], 16)

            def first_loads():
                sp.wait_ge(edges_normed, STEPS)
                sp.wait_ge(edges_normed_act, STEPS)
                sp.wait_ge(xd_copied, STEPS)
                for p in range(2):
                    sp.wait_ge(xs_stored[p], 16 * (FULL // 2 + (1 - p)))
                    sp.wait_ge(x1_stored[p], 16 * (FULL // 2 - 1))
                for c in (1, 0):
                    load_ys(step(c))
                    load_yd(step(c))
                    load_ew(step(c))
                for c in (1, 0):
                    sp.wait_ge(gaps_ok, STEPS - c)
                    load_restart(step(c), restartB_loaded)

            run(sp, phase_a)

            sp.wait_ge(ysB_normed, 1)
            load_ys(step(2))
            sp.wait_ge(ydB_normed, 1)
            sp.wait_ge(ydB_kept, 1)
            load_yd(step(2))
            for p in range(2):
                sp.wait_ge(out_stored[p], 16 * (FULL // 2 + (1 - p)))
            sp.sem_inc(out_all_stored, 1)

            def phase_b(s):
                far, farther = step(s, 2), step(s, 3)
                if farther:
                    sp.wait_ge(ysB_normed, s.c + 2)
                    open_gate()
                    load_ys(farther)
                    sp.wait_ge(ydB_normed, s.c + 2)
                    sp.wait_ge(ydB_kept, s.c + 2)
                    open_gate()
                    load_yd(farther)
                if far:
                    sp.wait_ge(msg_ok, s.c + 1)
                    open_gate()
                    load_ew(far)
                    sp.wait_ge(top_ok, s.c + 1)
                    open_gate()
                    load_restart(far, restartB_loaded)

            run(sp, phase_b, LOOPS_B)
            for p in range(2):
                uses = FULL // 2 + (1 - p)
                sp.wait_ge(out_put[p], 16 * ET * uses)

        @block.gpsimd
        def _(pool):
            pool.memset(prev_l[:, :], -1)
            pool.memset(next_i[:, :, :], -1).then_inc(consts_pool, 1)
            pool.memset(no_rows[:, :], NO_ROW).then_inc(no_rows_ready, 1)
            pool.memset(ident[:, :], 0.0)
            pool.memset(head_sum[:, :], 1.0).then_inc(consts_pool, 1)
            pool.iota(edge_i[:, 0:FULL, :], pattern=[[EC, FULL], [1, ET]], base=0, channel_multiplier=ET)
            pool.iota(edge_i[:, FULL, :], pattern=[[1, ET]], base=E - EC, channel_multiplier=ET).then_inc(consts_pool, 1)
            pool.wait_ge(consts_pool, 3)
            pool.affine_select(out=ident[:, :], in_=ident[:, :], compare_op=ALU.not_equal, fill=1.0,
                               base=0, pattern=[[-1, P]], channel_multiplier=1).then_inc(consts_pool, 1)
            blocks = head_sum[:, :].rearrange("p (g r) -> p g r", r=CH)
            pool.affine_select(out=blocks, in_=blocks, compare_op=ALU.is_ge, fill=0.0, base=0,
                               pattern=[[-CH, HEADS], [0, CH]], channel_multiplier=1).then_inc(consts_pool, 1)
            pool.wait_ge(consts_pool, 5)
            pool.affine_select(out=blocks, in_=blocks, compare_op=ALU.is_ge, fill=0.0, base=CH - 1,
                               pattern=[[CH, HEADS], [0, CH]], channel_multiplier=-1).then_inc(consts_pool, 1)

            def open_gate():
                pool.sem_inc(gate, 1)

            def gather(s, first):
                pool.wait_ge(ix_staged, s.c + 1)
                for rows, which, got in ((xs, 0, xs_got), (xd, 1, xd_got)):
                    if not first:
                        if rows is xs:
                            pool.wait_ge(edges_normed_act, s.c - 1)
                            pool.wait_ge(xs_stored[s.par], 16 * s.i)
                        else:
                            pool.wait_ge(edges_normed, s.c - 1)
                            pool.wait_ge(xd_copied, s.c - 1)
                    open_gate()
                    for j in range(ET):
                        pool.indirect_dma_start(
                            out=rows[:, s.par, j], out_offset=None, in_=x,
                            in_offset=bass.IndirectOffsetOnAxis(ap=gather_ix[:, s.par, which, j:j + 1].bitcast(U32), axis=0),
                        ).then_inc(got[s.par], 16)

            gather(step(0), True)
            gather(step(1), True)
            gather(step(2), False)

            def table_columns(a, first, width):
                return a[:, bass.ds(first, width), :].rearrange("p a j -> p (a j)")

            def put_entries(k, uses, n, first, width):
                cols_ = width * ET
                pool.wait_ge(table_put[k], 16 * uses)
                open_gate()
                pool.tensor_copy(table_ix[:, k, 0, 0:cols_], table_columns(end_i, first, width))
                pool.tensor_copy(table_ix[:, k, 1, 0:cols_], table_columns(edge_i, first, width)).then_inc(table_staged, 1)
                pool.wait_ge(table_staged, n + 1)
                open_gate()
                for j in range(cols_):
                    pool.indirect_dma_start(
                        out=last_edge, out_offset=bass.IndirectOffsetOnAxis(
                            ap=table_ix[:, k, 0, j:j + 1].bitcast(U32), axis=0),
                        in_=table_ix[:, k, 1, j:j + 1], in_offset=None,
                        bounds_check=N - 1, oob_is_err=False).then_inc(table_put[k], 16)

            def read_entries(k, uses, n, first, width):
                cols_ = width * ET
                pool.wait_ge(table_read[k], 16 * uses)
                open_gate()
                pool.tensor_copy(table_ix[:, k, 0, 0:cols_].rearrange("p (a j) -> p a j", j=ET),
                                 src_i[:, bass.ds(first, width), :]).then_inc(table_staged, 1)
                pool.wait_ge(table_staged, n + 1)
                open_gate()
                for j in range(cols_):
                    pool.indirect_dma_start(
                        out=table_got[:, k, j:j + 1], out_offset=None, in_=last_edge,
                        in_offset=bass.IndirectOffsetOnAxis(ap=table_ix[:, k, 0, j:j + 1].bitcast(U32), axis=0),
                    ).then_inc(table_read[k], 16)

            def keep_entries(k, uses, first, width):
                cols_ = width * ET
                pool.wait_ge(table_read[k], 16 * uses)
                open_gate()
                pool.tensor_copy(table_columns(found, first, width), table_got[:, k, 0:cols_]).then_inc(found_kept, 1)

            def phase_a(s, table_work):
                farther = step(s, 3)
                if farther:
                    gather(farther, False)
                table_work(s)

            FIRST_PUT = 0
            LAST_PUT = FIRST_PUT + FULL // 2
            FIRST_READ = LAST_PUT + 1
            assert FIRST_PUT % 2 == 0 and LAST_PUT % 2 == 0
            i0 = FIRST_PUT // 2
            i1 = FIRST_READ // 2
            PUTS = 2 * ET * (i1 - i0)

            def puts(s):
                put_entries(s.par, 2 * ET * (s.i - i0), s.c - FIRST_PUT, (s.c - FIRST_PUT) * 2, 2)

            def last_puts(s):
                for p in range(2):
                    pool.wait_ge(table_put[p], 16 * PUTS)
                put_entries(0, PUTS, s.c - FIRST_PUT, FULL, 1)

            def keep_last(s):
                keep_entries(1 - s.par, 2 * ET * (s.i - i1), (s.c - FIRST_READ) * 2 - 2, 2)

            def reads(s):
                if isinstance(s.i, int) and s.c == FIRST_READ:
                    pool.wait_ge(table_put[0], 16 * (PUTS + ET))
                else:
                    keep_last(s)
                read_entries(s.par, 2 * ET * (s.i - i1 - 1 + s.par), s.c - FIRST_PUT, (s.c - FIRST_READ) * 2, 2)

            for c in range(FIRST_PUT):
                gather(step(c, 3), False)
            pool.wait_ge(ends_ready, 2)
            pool.wait_ge(table_cleared, 16)
            for c in range(FIRST_PUT, FIRST_PUT + 2):
                phase_a(step(c), puts)
            with pool.Fori(i0 + 1, i1) as i:
                for par in range(2):
                    phase_a(Step(i, par, False, E, N), puts)
            phase_a(step(LAST_PUT), last_puts)
            for c in range(FIRST_READ, FIRST_READ + 3):
                phase_a(step(c), reads)
            with pool.Fori(i1 + 2, LOOPS) as i:
                for par in range(2):
                    phase_a(Step(i, par, False, E, N), reads)
            for c in range(2 * LOOPS, STEPS):
                phase_a(step(c), reads)
            c, first = STEPS, 2 * (STEPS - FIRST_READ)
            keep_last(Step(c // 2, c % 2, False, E, N))
            uses = [2 * ET * sum(1 for n in range(FIRST_READ, STEPS) if n % 2 == p) for p in range(2)]
            behind = None
            while first < FULL:
                read_entries(c % 2, uses[c % 2], c - FIRST_PUT, first, 2)
                uses[c % 2] += 2 * ET
                if behind:
                    keep_entries(*behind)
                behind = (c % 2, uses[c % 2], first, 2)
                c, first = c + 1, first + 2
            if behind:
                keep_entries(*behind)
            assert c - FIRST_READ == TABLE_KEPT

            def replace_rows(s):
                pool.wait_ge(ixB_staged, s.c + 1)
                pool.wait_ge(ys_loaded[s.par], 16 * (s.i + 1))
                open_gate()
                for j in range(ET):
                    pool.indirect_dma_start(
                        out=xs[:, s.par, j], out_offset=None, in_=x1_rows,
                        in_offset=bass.IndirectOffsetOnAxis(ap=gather_ix[:, s.par, 0, j:j + 1].bitcast(U32), axis=0),
                        bounds_check=E - 1, oob_is_err=False).then_inc(ys_replaced[s.par], 16)

            def put_rows(s):
                pool.wait_ge(row_ok, s.c + 1)
                if isinstance(s.i, int) and s.c == 0:
                    pool.wait_ge(out_all_stored, 1)
                if s.last:
                    pool.wait_ge(out_put[1 - s.par], 16 * ET * s.i)
                open_gate()
                for j in range(ET):
                    pool.indirect_dma_start(
                        out=out, out_offset=bass.IndirectOffsetOnAxis(
                            ap=gather_ix[:, s.par, 1, j:j + 1].bitcast(U32), axis=0),
                        in_=x1[:, s.par, j], in_offset=None,
                        bounds_check=N - 1, oob_is_err=False).then_inc(out_put[s.par], 16)

            pool.wait_ge(x1_all_stored, 1)
            open_gate()
            replace_rows(step(0))
            replace_rows(step(1))
            read_entries(c % 2, uses[c % 2], c - FIRST_PUT, FULL, 1)
            keep_entries(c % 2, uses[c % 2] + ET, FULL, 1)
            replace_rows(step(2))

            def phase_b(s):
                farther = step(s, 3)
                if farther:
                    replace_rows(farther)
                put_rows(s)

            run(pool, phase_b, LOOPS_B)

        @block.vector
        def _(dve):
            def row_of(s, t):
                return (x_in[:, s.par, t] if t < NT else xs[:, s.par, t - NT] if t < NT + ET
                        else xd[:, s.par, t - NT - ET])

            dve.memset(ones_bf[:, :], 1.0)
            dve.memset(b2_rows[:, :], 0.0)
            dve.memset(carry[:, :], 0.0)
            dve.memset(den[:, :, :], 0.0)
            dve.memset(acc[:, :, :], 0.0)
            dve.memset(top[:, :, :], 0.0)
            dve.memset(WeT[:, :, :], 0.0).then_inc(consts_dve, 1)
            def stage_gather(s):
                dve.tensor_copy(gather_ix[:, s.par], edge_ix[:, bass.ds(s.c, 1)].rearrange("p a w j -> p (a w) j")
                                ).then_inc(ix_staged, 1)

            dve.wait_ge(ix_in, 4 * 16)
            stage_gather(step(0))
            stage_gather(step(1))
            dve.wait_ge(l_in, 3 * 16)
            dve.tensor_tensor(restart_l[:, :], dst_l[:, :], prev_l[:, :], ALU.not_equal).then_inc(ends_found, 1)
            dve.wait_ge(ends_found, 1)
            dve.tensor_scalar(restart_l[:, :], restart_l[:, :], NEG, None, ALU.mult).then_inc(restart_ready, 1)
            dve.wait_ge(next_in, 3 * 16)
            dve.tensor_tensor(inner[:, :, :], dst_i[:, :, :], next_i[:, :, :], ALU.is_equal).then_inc(ends_ready, 1)
            dve.wait_ge(ends_ready, 1)
            dve.scalar_tensor_tensor(end_i[:, :, :], inner[:, :, :], float(NO_ROW), dst_i[:, :, :],
                                     ALU.mult, ALU.add).then_inc(ends_ready, 1)
            dve.wait_ge(b2_in, 16)
            for k in range(1, 4):
                dve.tensor_copy(b2_rep[:, k * D:(k + 1) * D], b2_rep[:, 0:D]).then_inc(b2_split, 1)
            dve.wait_ge(b2_split, 3)
            dve.tensor_copy(b2_part[:, 0], b2_rep[:, :]).then_inc(b2_split, 1)
            dve.wait_ge(b2_split, 4)
            dve.tensor_tensor(b2_rest[:, 0], b2_rep[:, :], b2_part[:, 0], ALU.subtract).then_inc(b2_split, 1)
            dve.wait_ge(b2_split, 5)
            dve.tensor_copy(b2_part[:, 1], b2_rest[:, 0]).then_inc(b2_split, 1)
            dve.wait_ge(b2_split, 6)
            dve.tensor_tensor(b2_rest[:, 1], b2_rest[:, 0], b2_part[:, 1], ALU.subtract).then_inc(b2_split, 1)
            dve.wait_ge(b2_split, 7)
            dve.tensor_copy(b2_part[:, 2], b2_rest[:, 1]).then_inc(b2_split, 1)
            dve.wait_ge(b2_split, 8)
            dve.wait_ge(consts_dve, 1)
            for k in range(3):
                dve.tensor_copy(b2_rows[32 * k:32 * k + 1, :], b2_part[32 * k:32 * k + 1, k]).then_inc(b2_split, 1)
            dve.wait_ge(setup_ps, 1)
            dve.tensor_scalar(WqT[:, :], E0[:, 0:P], 1.0 / np.sqrt(CH), None, ALU.mult)
            for k, w in enumerate((WkT, WvT, WdT)):
                dve.tensor_copy(w[:, :], E0[:, (k + 1) * P:(k + 2) * P])
            for j in range(ET):
                last = dve.tensor_copy(WeT[KA * j:KA * (j + 1), j], E1[KA * j:KA * (j + 1), 0:P])
            last.then_inc(setup_sb, 1)
            dve.wait_ge(setup_ps, 2)
            dve.tensor_tensor(Wh[:, :], E2[:, 0:P], W1a[:, :], ALU.add)
            dve.wait_ge(col_in, 3 * 16)
            dve.tensor_tensor(cols[:, 3:4], E3[:, 0:1], cols[:, 1:2], ALU.add).then_inc(setup_sb, 1)

            def norm_stats(row, tiles):
                for t in tiles:
                    ins = dve.bn_stats(stats[:, t], row(t))
                return ins

            ROOT0 = 4
            LAST = ROOT0 + 3 * ROOT_STEPS

            def scales(stage, mine, batch, p, a, b, free=()):
                w = slice(a, b)
                dve.wait_ge(mine, batch * LAST + stage + 1)
                if stage == 0:
                    m0, m1, v0, v1 = stats[:, w, 1], stats[:, w, 4], stats[:, w, 2], stats[:, w, 5]
                    dve.tensor_tensor(sums[:, w], m0, m1, ALU.add)
                    dve.tensor_tensor(diff[:, w], m0, m1, ALU.subtract)
                    ins = dve.scalar_tensor_tensor(q4[:, w], v0, EPS * D, v1, ALU.add, ALU.add)
                elif stage == 1:
                    ins = dve.scalar_tensor_tensor(sq[:, w], diff[:, w], 0.25, diff[:, w], ALU.mult, ALU.mult)
                elif stage == 2:
                    ins = dve.scalar_tensor_tensor(var[:, w], q4[:, w], 1.0 / D, sq[:, w], ALU.mult, ALU.add)
                elif stage == 3:
                    dve.tensor_scalar(guess[:, w].bitcast(I32), var[:, w].bitcast(I32), 1, None,
                                      ALU.logical_shift_right).then_inc(half_ok, 1)
                    dve.wait_ge(half_ok, batch + 1 + (STEPS + 1 if mine is lnB else 0))
                    ins = dve.tensor_scalar(root[:, w].bitcast(I32), guess[:, w].bitcast(I32), -1.0,
                                            float(ROOT_BITS), ALU.mult, ALU.add)
                elif (stage - ROOT0) % 3 == 0:
                    ins = dve.tensor_tensor(root_t[:, w], root[:, w], root[:, w], ALU.mult)
                elif (stage - ROOT0) % 3 == 1:
                    ins = dve.scalar_tensor_tensor(root_u[:, w], root_t[:, w], -0.5, var[:, w], ALU.mult, ALU.mult)
                else:
                    y = root[:, w]
                    if stage == LAST - 1:
                        y = rstd[:, p, w]
                        for sem_, n in free:
                            dve.wait_ge(sem_, n)
                    ins = dve.scalar_tensor_tensor(y, root_u[:, w], 1.5, root[:, w], ALU.add, ALU.mult)
                if stage < LAST - 1:
                    ins.then_inc(mine, 1)
                else:
                    ins.then_inc(root_ok, 1)

            def shifts(done, roots, p, a, b):
                w = slice(a, b)
                dve.wait_ge(root_ok, roots)
                dve.scalar_tensor_tensor(shift[:, p, w], sums[:, w], -0.5, rstd[:, p, w],
                                         ALU.mult, ALU.mult).then_inc(done, 1)

            def norm_rows(s, tiles, row):
                for t in tiles:
                    ins = dve.tensor_scalar(h[:, s.par, t], row(t), rstd[:, s.par, t:t + 1], shift[:, s.par, t:t + 1],
                                            ALU.mult, ALU.add)
                return ins

            edge_tiles = range(NT, NL)
            dve_tiles = range(ACT_TILES, NL)

            def edge_stats(s):
                dve.wait_ge(xs_got[s.par], 16 * ET * (s.i + 1))
                dve.wait_ge(xd_got[s.par], 16 * ET * (s.i + 1))
                return norm_stats(lambda t: row_of(s, t), edge_tiles)

            def node_stats(s, halves=range(2)):
                for half in halves:
                    dve.wait_ge(x_loaded[half][s.par], 16 * (s.i + 1))
                    ins = norm_stats(lambda t: row_of(s, t), range(half * NT // 2, (half + 1) * NT // 2))
                return ins

            def edge_rows(s):
                norm_rows(s, dve_tiles, lambda t: row_of(s, t)).then_inc(edges_normed, 1)

            def products(s):
                dve.wait_ge(k_ps, s.c + 1)
                dve.wait_ge(q_ok, s.c + 1)
                dve.wait_ge(s_ps, s.c)
                dve.tensor_tensor(qk[:, :], q_sb[:, :], E2[:, :], ALU.mult).then_inc(qk_ok, 1)

            node_stats(step(0))
            edge_stats(step(0)).then_inc(ln, 1)
            for k in range(LAST):
                scales(k, ln, 0, 0, NT, NL)
            stage_gather(step(2))
            shifts(scales_ready, 1, 0, NT, NL)
            dve.wait_ge(scales_ready, 1)
            edge_rows(step(0))
            edge_stats(step(1)).then_inc(ln, 1)
            for k in range(LAST):
                scales(k, ln, 1, 1, 0, NL)
            shifts(scales_ready, 2, 1, 0, NL)
            dve.wait_ge(scales_ready, 2)
            edge_rows(step(1))
            products(step(0))
            edge_stats(step(2))
            node_stats(step(1), [0])

            def add_rows(s, k):
                if k == 0:
                    dve.wait_ge(out_stored[s.par], 16 * s.i)
                dve.wait_ge(o_ps, DT * s.c + k + 1)
                dve.tensor_tensor(x_out[:, s.par, ET * k:ET * (k + 1)],
                                  O_ps[:, :].rearrange("p (j d) -> p j d", j=ET),
                                  x_in[:, s.par, ET * k:ET * (k + 1)], ALU.add).then_inc(out_ok, 1)

            SEAM = FULL * EC - (E - EC)

            def phase_a(s):
                nxt, far, farther = step(s, 1), step(s, 2), step(s, 3)
                before = EC - 1 - SEAM if s.last else EC - 1
                seam = EC - 1 - SEAM if isinstance(s.i, int) and s.c == FULL - 1 else EC - 1
                tiles = (0 if nxt else NT, NL if far else NT)

                def scale(*stages):
                    for k in stages:
                        if nxt:
                            scales(k, ln, s.c + 2, s.par, *tiles, free=[(nodes_normed, DT * s.c), (edges_normed_act, s.c + 1)])

                if farther:
                    stage_gather(farther)
                dve.wait_ge(s_ok, s.c + 1)
                dve.wait_ge(restart_loaded[s.par], 16 * (s.i + 1))
                dve.wait_ge(carried, s.c)
                dve.wait_ge(rden_ok, s.c)
                dve.tensor_tensor_scan(E3[:, :], restart[:, s.par], s_sb[:, :], carry[:, 0:1],
                                       ALU.add, ALU.max).then_inc(max_ok, 1)
                dve.wait_ge(max_ok, s.c + 1)
                dve.tensor_tensor(ga[:, 0:1], restart[:, s.par, 0:1], carry[:, 0:1], ALU.add)
                dve.tensor_tensor(ga[:, 1:EC], restart[:, s.par, 1:EC], E3[:, 0:EC - 1], ALU.add).then_inc(gap0_ok, 1)
                dve.tensor_tensor(gb[:, :], s_sb[:, :], E3[:, :], ALU.subtract)
                dve.wait_ge(gap0_ok, s.c + 1)
                dve.tensor_copy(carry[:, 0:1], E3[:, seam:seam + 1]).then_inc(carried, 1)
                dve.tensor_tensor(ga[:, :], ga[:, :], E3[:, :], ALU.subtract).then_inc(gaps_ok, 1)
                if nxt:
                    node_stats(nxt, [1]).then_inc(ln, 1)
                add_rows(s, 0)
                scale(0)
                if nxt:
                    products(nxt)
                scale(1, 2)
                dve.wait_ge(exp_ok, s.c + 1)
                dve.tensor_tensor_scan(den[:, s.par], ga[:, :], gb[:, :], den[:, 1 - s.par, before:before + 1],
                                       ALU.mult, ALU.add).then_inc(den_ok, 1)
                scale(3)
                dve.wait_ge(v_ps, s.c + 1)
                dve.tensor_tensor(bv[:, :], gb[:, :], E4[:, :], ALU.mult).then_inc(bv_ok, 1)
                scale(4)
                dve.wait_ge(bv_ok, s.c + 1)
                dve.tensor_tensor_scan(acc[:, s.par], ga[:, :], bv[:, :], acc[:, 1 - s.par, before:before + 1],
                                       ALU.mult, ALU.add).then_inc(acc_ok, 1)
                scale(5, 6)
                add_rows(s, 1)
                scale(7, 8)
                dve.wait_ge(den_ps, s.c + 1)
                dve.reciprocal(rden[:, :, :], E3[:, :].rearrange("p (j g r) -> p j g r", j=ET, r=CH)[:, :, :, 0]
                               ).then_inc(rden_ok, 1)
                scale(9)
                dve.wait_ge(rden_ok, s.c + 1)
                dve.wait_ge(acc_ps, s.c + 1)
                heads = E4[:, :].rearrange("p (g r) -> p g r", r=CH)
                dve.tensor_tensor(heads, heads, rden[:, :, :].rearrange("p j g -> p (j g)").unsqueeze(2)
                                  .broadcast_to([P, ET * HEADS, CH]), ALU.mult).then_inc(att_ok, 1)
                scale(*range(10, LAST))
                if nxt:
                    shifts(scales_ready, s.c + 3, s.par, *tiles)
                dve.wait_ge(att_ok, s.c + 1)
                dve.wait_ge(xd_copied, s.c + 1)
                dve.wait_ge(x1_stored[s.par], 16 * s.i)
                dve.tensor_tensor(x1[:, s.par], E4[:, :].rearrange("p (j d) -> p j d", j=ET),
                                  xd_kept[:, s.par], ALU.add).then_inc(x1_ok, 1)
                if far:
                    dve.wait_ge(scales_ready, s.c + 3)
                    dve.wait_ge(hdT_ps, s.c + 1)
                    edge_rows(far)
                add_rows(s, 2)
                if farther:
                    edge_stats(farther)
                add_rows(s, 3)
                if far:
                    node_stats(far, [0])

            run(dve, phase_a)

            def stats_b(s):
                dve.wait_ge(ys_replaced[s.par], 16 * ET * (s.i + 1))
                dve.wait_ge(yd_loaded[s.par], 16 * (s.i + 1))
                norm_stats(lambda t: row_of(s, t), edge_tiles).then_inc(lnB, 1)

            def rows_b(s):
                dve.wait_ge(scalesB, s.c + 1)
                norm_rows(s, range(NT + ET, NL), lambda t: row_of(s, t)).then_inc(ydB_normed, 1)

            def stage_found(s):
                dve.tensor_copy(gather_ix[:, s.par, 0], found[:, bass.ds(s.c, 1), :].rearrange("p a j -> p (a j)")
                                ).then_inc(ixB_staged, 1)

            A_BATCHES = STEPS + 1
            dve.wait_ge(found_kept, TABLE_KEPT)
            stage_found(step(0))
            stage_found(step(1))
            for c in range(2):
                stats_b(step(c))
                if c == 0:
                    stage_found(step(2))
                for k in range(LAST):
                    scales(k, lnB, c, c, NT, NL)
                shifts(scalesB, A_BATCHES + c + 1, c, NT, NL)
                rows_b(step(c))

            def phase_b(s):
                far, farther = step(s, 2), step(s, 3)
                before = EC - 1 - SEAM if s.last else EC - 1

                def scale(*stages):
                    for k in stages:
                        if far:
                            scales(k, lnB, s.c + 2, s.par, NT, NL, [(ysB_normed, s.c + 1)])

                if isinstance(s.i, int) and s.c == 0:
                    dve.wait_ge(found_kept, TABLE_KEPT + 1)
                if farther:
                    stage_found(farther)
                dve.wait_ge(m_ps, s.c + 1)
                dve.wait_ge(ew_loaded[s.par], 16 * (s.i + 1))
                dve.scalar_tensor_tensor(msg[:, :], ew[:, s.par], cols[:, 2:3], E2[:, :],
                                         ALU.mult, ALU.add).then_inc(msg_ok, 1)
                dve.wait_ge(msg_ok, s.c + 1)
                dve.wait_ge(restartB_loaded[s.par], 16 * (s.i + 1))
                dve.wait_ge(g_ps, s.c)
                dve.tensor_tensor_scan(top[:, s.par], restart[:, s.par], msg[:, :], top[:, 1 - s.par, before:before + 1],
                                       ALU.add, ALU.max).then_inc(top_ok, 1)
                if far:
                    stats_b(far)
                scale(*range(LAST))
                if far:
                    shifts(scalesB, A_BATCHES + s.c + 3, s.par, NT, NL)
                    dve.wait_ge(ydT_ps, s.c + 1)
                    rows_b(far)
                dve.wait_ge(out_put[s.par], 16 * ET * s.i)
                dve.tensor_copy(gather_ix[:, s.par, 1], end_i[:, bass.ds(s.c, 1), :].rearrange("p a j -> p (a j)"))
                dve.wait_ge(r_ps, s.c + 1)
                dve.wait_ge(ydB_kept, s.c + 1)
                dve.tensor_tensor(x1[:, s.par], E4[:, :].rearrange("p (j d) -> p j d", j=ET),
                                  xd_kept[:, s.par], ALU.add).then_inc(row_ok, 1)

            run(dve, phase_b, LOOPS_B)

        @block.scalar
        def _(act):
            def turned(dst_tile, src_bank, func=ACT.Relu):
                return act.activation(dst_tile.rearrange("f (p j) -> f j p", j=ET),
                                      src_bank[:, :].rearrange("f (j p) -> f j p", j=ET), func)

            def normalise(s, tiles, p):
                for t in tiles:
                    row = (x_in[:, s.par, t] if t < NT else xs[:, s.par, t - NT] if t < NT + ET
                           else xd[:, s.par, t - NT - ET])
                    ins = act.activation(h[:, s.par, t], row, ACT.Relu, bias=shift[:, p, t:t + 1],
                                         scale=rstd[:, p, t:t + 1])
                return ins

            def keep_xd(s):
                act.wait_ge(xd_got[s.par], 16 * ET * (s.i + 1))
                act.activation(xd_kept[:, s.par], xd[:, s.par], ACT.Copy).then_inc(xd_copied, 1)

            act_edges = range(NT, ACT_TILES)

            def edge_columns(s):
                act.wait_ge(hsT_ps, s.c + 1)
                if not (isinstance(s.i, int) and s.c == 0):
                    act.wait_ge(v_ps, s.c - 1)
                turned(hsT[:, s.par], E0).then_inc(hsT_ok, 1)
                act.wait_ge(hdT_ps, s.c + 1)
                act.wait_ge(q_ps, s.c)
                turned(hdT[:, 0], E1).then_inc(hdT_ok, 1)
                act.wait_ge(attrT_ps, s.c + 1)
                act.wait_ge(s_ps, s.c)
                act.activation(attrT[:, :], E2[:, 0:P], ACT.Copy).then_inc(attrT_ok, 1)

            def queries(s):
                act.wait_ge(q_ps, s.c + 1)
                act.wait_ge(qk_ok, s.c)
                act.activation(q_sb[:, :], E1[:, :], ACT.Copy).then_inc(q_ok, 1)

            def scores(s):
                act.wait_ge(s_ps, s.c + 1)
                act.wait_ge(gaps_ok, s.c)
                act.activation(s_sb[:, :], E0[:, :], ACT.Copy).then_inc(s_ok, 1)

            def part(s, k):
                normalise(s, range(ET * k, ET * (k + 1)), 1 - s.par).then_inc(nodes_normed, 1)

            act.wait_ge(scales_ready, 1)
            normalise(step(0), act_edges, 0).then_inc(edges_normed_act, 1)
            keep_xd(step(0))
            edge_columns(step(0))
            queries(step(0))
            act.wait_ge(scales_ready, 2)
            part(step(0), 0)
            normalise(step(1), act_edges, 1).then_inc(edges_normed_act, 1)
            scores(step(0))
            keep_xd(step(1))

            def phase_a(s):
                nxt, far = step(s, 1), step(s, 2)

                def evac_h(k):
                    n = DT * s.c + k
                    act.wait_ge(hT_ps, n + 1)
                    act.wait_ge(hid_ps, n - 1 if k else n)
                    act.activation(hT[:, k % 2], T_ps[:, :], ACT.Relu).then_inc(hT_ok, 1)

                def evac_hid(k):
                    n = DT * s.c + k
                    act.wait_ge(hid_ps, n + 1)
                    act.wait_ge(o_ps, n - 1 if k else n)
                    act.activation(hid[:, k % 2], H_ps[:, :], ACT.Relu, bias=cols[:, 1:2]).then_inc(hid_ok, 1)

                evac_h(0)
                if nxt:
                    edge_columns(nxt)
                part(s, 1)
                evac_hid(0)
                act.wait_ge(gaps_ok, s.c + 1)
                act.activation(ga[:, :], ga[:, :], ACT.Exp)
                act.activation(gb[:, :], gb[:, :], ACT.Exp).then_inc(exp_ok, 1)
                evac_h(1)
                if nxt:
                    queries(nxt)
                part(s, 2)
                evac_hid(1)
                evac_h(2)
                part(s, 3)
                evac_hid(2)
                evac_h(3)
                if nxt:
                    act.wait_ge(scales_ready, s.c + 3)
                    act.wait_ge(hT_ps, DT * s.c)
                    part(nxt, 0)
                evac_hid(3)
                if nxt:
                    scores(nxt)
                if far:
                    act.wait_ge(hdT_ps, s.c + 1)
                    normalise(far, act_edges, s.par).then_inc(edges_normed_act, 1)
                    act.wait_ge(x1_ok, s.c + 1)
                    keep_xd(far)

            run(act, phase_a)

            def columns_b(s):
                act.wait_ge(ysT_ps, s.c + 1)
                act.wait_ge(m_ps, s.c)
                turned(hsT[:, 0], E0).then_inc(ysT_ok, 1)
                act.wait_ge(ydT_ps, s.c + 1)
                if not (isinstance(s.i, int) and s.c == 0):
                    act.wait_ge(g_ps, s.c - 1)
                turned(hdT[:, s.par], E1).then_inc(ydT_ok, 1)

            def keep_yd(s):
                act.wait_ge(yd_loaded[s.par], 16 * (s.i + 1))
                act.activation(xd_kept[:, s.par], xd[:, s.par], ACT.Copy).then_inc(ydB_kept, 1)

            act.wait_ge(x1_ok, STEPS)
            keep_yd(step(0))
            for c in range(2):
                act.wait_ge(scalesB, c + 1)
                normalise(step(c), range(NT, NT + ET), c).then_inc(ysB_normed, 1)
            columns_b(step(0))

            def phase_b(s):
                nxt, far = step(s, 1), step(s, 2)
                if nxt:
                    columns_b(nxt)
                    act.wait_ge(row_ok, s.c)
                    keep_yd(nxt)
                act.wait_ge(g_ps, s.c + 1)
                act.wait_ge(r_ps, s.c)
                act.activation(hidB[:, :], E3[:, :], ACT.Relu, bias=cols[:, 3:4]).then_inc(g_ok, 1)
                if far:
                    act.wait_ge(scalesB, s.c + 3)
                    act.wait_ge(ysT_ps, s.c + 1)
                    normalise(far, range(NT, NT + ET), s.par).then_inc(ysB_normed, 1)

            run(act, phase_b, LOOPS_B)

        @block.tensor
        def _(pe):
            pe.wait_ge(consts_pool, 6)
            pe.wait_ge(w_in, 16 * 16)
            for n in range(4):
                pe.transpose(E0[:, n * P:(n + 1) * P], wload[:, n], ident[:, :])
            pe.transpose(E1[:, 0:P], we_rows[:, :, :].rearrange("p j k -> p (j k)"), ident[:, :]).then_inc(setup_ps, 1)
            pe.wait_ge(setup_sb, 1)
            pe.wait_ge(col_in, 3 * 16)
            pe.matmul(E2[:, 0:P], WdT[:, :], W1b[:, :], start=True, stop=True)
            pe.matmul(E3[:, 0:1], W1b[:, :], cols[:, 0:1], start=True, stop=True).then_inc(setup_ps, 1)
            pe.wait_ge(setup_sb, 2)

            def turn(bank_, s, first):
                for j in range(ET):
                    ins = pe.transpose(bank_[:, j * P:(j + 1) * P], h[:, s.par, first + j], ident[:, :])
                return ins

            def rows_out(bank_, hidden):
                pe.matmul(bank_[:, :], ones_bf[:, :], b2_rows[:, :], start=True, stop=False, skip_group_check=True)
                for j in range(ET):
                    ins = pe.matmul(bank_[:, j * P:(j + 1) * P], hidden(j), W2s[:, :],
                                    start=False, stop=True, skip_group_check=True)
                return ins

            def edge_columns(s):
                pe.wait_ge(edges_normed, s.c + 1)
                pe.wait_ge(edges_normed_act, s.c + 1)
                pe.wait_ge(s_ok, s.c)
                turn(E0, s, NT).then_inc(hsT_ps, 1)
                pe.wait_ge(q_ok, s.c)
                turn(E1, s, NT + ET).then_inc(hdT_ps, 1)
                pe.wait_ge(attr_loaded[s.par], 16 * (s.i + 1))
                pe.wait_ge(qk_ok, s.c)
                pe.transpose(E2[:, 0:P], attr[:, s.par].rearrange("p j k -> p (j k)"), ident[:, :]).then_inc(attrT_ps, 1)

            def queries_keys(s):
                pe.wait_ge(hdT_ok, s.c + 1)
                pe.matmul(E1[:, :], WqT[:, :], hdT[:, 0], start=True, stop=True).then_inc(q_ps, 1)
                pe.wait_ge(hsT_ok, s.c + 1)
                pe.wait_ge(attrT_ok, s.c + 1)
                pe.matmul(E2[:, :], WkT[:, :], hsT[:, s.par], start=True, stop=True).then_inc(k_ps, 1)

            def scores(s):
                pe.wait_ge(qk_ok, s.c + 1)
                pe.matmul(E0[:, :], head_sum[:, :], qk[:, :], start=True, stop=False, skip_group_check=True)
                for j in range(ET):
                    ins = pe.matmul(E0[:, j::ET], WeT[:, j], attrT[:, :], start=False, stop=True, skip_group_check=True)
                ins.then_inc(s_ps, 1)

            edge_columns(step(0))
            queries_keys(step(0))
            scores(step(0))

            def phase_a(s):
                nxt = step(s, 1)

                def turn_h(k):
                    pe.wait_ge(nodes_normed, DT * s.c + k + 1)
                    pe.wait_ge(hT_ok, DT * s.c + k)
                    turn(T_ps, s, ET * k).then_inc(hT_ps, 1)

                def hidden(k):
                    n = DT * s.c + k
                    pe.wait_ge(hT_ok, n + 1)
                    pe.wait_ge(hid_ok, n)
                    pe.matmul(H_ps[:, :], W1a[:, :], hT[:, k % 2], start=True, stop=True).then_inc(hid_ps, 1)

                def second(k):
                    n = DT * s.c + k
                    pe.wait_ge(hid_ok, n + 1)
                    pe.wait_ge(out_ok, n)
                    rows_out(O_ps, lambda j: hid[:, k % 2, j * P:(j + 1) * P]).then_inc(o_ps, 1)

                pe.wait_ge(x1_ok, s.c)
                pe.wait_ge(hsT_ok, s.c + 1)
                pe.matmul(E4[:, :], WvT[:, :], hsT[:, s.par], start=True, stop=True).then_inc(v_ps, 1)
                turn_h(0)
                if nxt:
                    edge_columns(nxt)
                hidden(0)
                if nxt:
                    queries_keys(nxt)
                turn_h(1)
                second(0)
                hidden(1)
                turn_h(2)
                second(1)
                hidden(2)
                pe.wait_ge(acc_ok, s.c + 1)
                for j in range(ET):
                    ins = pe.transpose(E3[:, j * P:(j + 1) * P], den[:, s.par, j::ET], ident[:, :])
                ins.then_inc(den_ps, 1)
                for j in range(ET):
                    ins = pe.transpose(E4[:, j * P:(j + 1) * P], acc[:, s.par, j::ET], ident[:, :])
                ins.then_inc(acc_ps, 1)
                turn_h(3)
                second(2)
                hidden(3)
                if nxt:
                    scores(nxt)
                second(3)

            pe.wait_ge(b2_split, 11)
            run(pe, phase_a)

            pe.wait_ge(x1_ok, STEPS)

            def columns_b(s):
                pe.wait_ge(ysB_normed, s.c + 1)
                pe.wait_ge(ysT_ok, s.c)
                turn(E0, s, NT).then_inc(ysT_ps, 1)
                pe.wait_ge(ydB_normed, s.c + 1)
                pe.wait_ge(ydT_ok, s.c)
                turn(E1, s, NT + ET).then_inc(ydT_ps, 1)

            def messages(s):
                pe.wait_ge(ysT_ok, s.c + 1)
                pe.wait_ge(msg_ok, s.c)
                pe.matmul(E2[:, :], Ws[:, :], hsT[:, 0], start=True, stop=True).then_inc(m_ps, 1)

            columns_b(step(0))
            messages(step(0))

            def phase_b(s):
                nxt = step(s, 1)
                if nxt:
                    columns_b(nxt)
                pe.wait_ge(ydT_ok, s.c + 1)
                pe.wait_ge(g_ok, s.c)
                pe.matmul(E3[:, :], Wh[:, :], hdT[:, s.par], start=True, stop=False)
                if nxt:
                    messages(nxt)
                pe.wait_ge(top_ok, s.c + 1)
                pe.matmul(E3[:, :], W1b[:, :], top[:, s.par], start=False, stop=True).then_inc(g_ps, 1)
                pe.wait_ge(g_ok, s.c + 1)
                pe.wait_ge(row_ok, s.c)
                rows_out(E4, lambda j: hidB[:, j::ET]).then_inc(r_ps, 1)

            run(pe, phase_b, LOOPS_B)


_INS = ["x", "src", "dst", "edge_attr_32", "edge_weight", "L0_gnn_Wq", "L0_gnn_Wk", "L0_gnn_Wv", "L0_gnn_We",
        "L1_gnn_Wm", "L1_gnn_bm", "L1_gnn_W1", "L1_gnn_b1", "L1_gnn_W2", "L1_gnn_b2"]


def kernel(**inputs):
    import concourse.bacc as bacc
    from concourse.bass_utils import run_bass_kernel_spmd

    nc = bacc.Bacc("TRN2", target_bir_lowering=False, num_devices=1)
    arrays, args = {}, []
    for name in _INS:
        a = np.ascontiguousarray(inputs[name])
        arrays[f"in_{name}"] = a
        args.append(nc.dram_tensor(f"in_{name}", a.shape, mybir.dt.from_np(a.dtype), kind="ExternalInput").ap())
    shape = inputs["x"].shape
    args.append(nc.dram_tensor("out_x", shape, F32, kind="ExternalOutput").ap())
    gnn_two_layers(nc, *args)
    return run_bass_kernel_spmd(nc, [arrays], core_ids=[0]).results[0]["out_x"]
```
